# Optimizing a Trainium2 kernel written in Bass

```python
import numpy as np
import jax
import jax.numpy as jnp

def _softmax(x, axis=-1):
    return jax.nn.softmax(x, axis=axis)

def _gelu(x):
    return jax.nn.gelu(x, approximate=True)

def _silu(x):
    return jax.nn.silu(x)

def _sigmoid(x):
    return jax.nn.sigmoid(x)

def _layernorm(x, axis=-1, eps=1e-05):
    m = jnp.mean(x, axis=axis, keepdims=True)
    v = jnp.var(x, axis=axis, keepdims=True)
    return (x - m) / jnp.sqrt(v + eps)

def _scatter_add(tgt, idx, src, axis=0):
    return tgt.at[idx].add(src)

def _segment_sum(src, seg, n):
    return jax.ops.segment_sum(src, seg, n)
kernel_name = 'mk_xattn_seq_d2_seqx_r2_84c247'

def setup_inputs(seed: int=0):
    np.random.seed(seed)
    _w = jnp.asarray

    def _rec_inputs():
        import jax
        import jax.numpy as jnp
        _rk = jax.random.key(seed)
        x = -0.0002928 + 1 * jax.random.normal(jax.random.fold_in(_rk, 1), (8, 224, 512), jnp.float32)
        _lenS = 224 - jax.random.randint(jax.random.fold_in(_rk, 7), (8,), 0, max(1, 224 // 4) + 1, jnp.int32)
        _lenS2 = 750 - jax.random.randint(jax.random.fold_in(_rk, 8), (8,), 0, max(1, 750 // 4) + 1, jnp.int32)
        _ctx_1024P = jax.random.normal(jax.random.fold_in(_rk, 11), (8, 16, 512), jnp.float32)
        _ctx_1024c = jax.random.dirichlet(jax.random.fold_in(_rk, 511), 0.3 * jnp.ones((16,), jnp.float32), (8, 750))
        _ctx_1024t = jnp.einsum('bsk,bkd->bsd', _ctx_1024c, _ctx_1024P)
        _ctx_1024t = _ctx_1024t * jax.lax.rsqrt(jnp.mean(jnp.square(_ctx_1024t)) + 1e-12) * 0.953939
        ctx_1024 = -1.39393e-06 + 0.999914 * (_ctx_1024t + 0.3 * jax.random.normal(jax.random.fold_in(_rk, 611), (8, 750, 512), jnp.float32))
        return (x, ctx_1024)
    x, ctx_1024 = _rec_inputs()

    def _L0_xattn_setup():
        import jax, jax.numpy as jnp
        import numpy as np
        D_MODEL = 512
        N_HEADS = 16
        D_K = D_MODEL // N_HEADS
        LN_EPS = 1e-05

        def _attention(query, key_value, W_qkv, b_qkv, W_o, b_o, ln_gamma, ln_beta):
            B, Sq, _ = query.shape
            Skv = key_value.shape[1]
            Wq, Wk, Wv = (W_qkv[:D_MODEL], W_qkv[D_MODEL:2 * D_MODEL], W_qkv[2 * D_MODEL:])
            bq, bk, bv = (b_qkv[:D_MODEL], b_qkv[D_MODEL:2 * D_MODEL], b_qkv[2 * D_MODEL:])
            Q = (query @ Wq.T + bq).reshape(B, Sq, N_HEADS, D_K).transpose(0, 2, 1, 3)
            K = (key_value @ Wk.T + bk).reshape(B, Skv, N_HEADS, D_K).transpose(0, 2, 1, 3)
            V = (key_value @ Wv.T + bv).reshape(B, Skv, N_HEADS, D_K).transpose(0, 2, 1, 3)
            scores = jnp.einsum('bhqd,bhkd->bhqk', Q.astype(jnp.float32), K.astype(jnp.float32))
            scores = scores / np.sqrt(D_K)
            attn = jax.nn.softmax(scores, axis=-1)
            context = jnp.einsum('bhqk,bhkd->bhqd', attn, V.astype(jnp.float32)).astype(query.dtype)
            context = context.transpose(0, 2, 1, 3).reshape(B, Sq, D_MODEL)
            output = context @ W_o.T + b_o
            x = output + query
            mu = jnp.mean(x, axis=-1, keepdims=True)
            var = jnp.mean(jnp.square(x - mu), axis=-1, keepdims=True)
            return (x - mu) / jnp.sqrt(var + LN_EPS) * ln_gamma + ln_beta
        key = jax.random.key(seed)
        ks = jax.random.split(key, 8)
        B, Sq, Skv = (2, 1024, 1024)
        scale = 1.0 / np.sqrt(D_MODEL)
        return {'query': jax.random.normal(ks[0], (B, Sq, D_MODEL), dtype=jnp.float32), 'key_value': jax.random.normal(ks[1], (B, Skv, D_MODEL), dtype=jnp.float32), 'W_qkv': jax.random.normal(ks[2], (3 * D_MODEL, D_MODEL), dtype=jnp.float32) * scale, 'b_qkv': jax.random.normal(ks[3], (3 * D_MODEL,), dtype=jnp.float32) * 0.01, 'W_o': jax.random.normal(ks[4], (D_MODEL, D_MODEL), dtype=jnp.float32) * scale, 'b_o': jax.random.normal(ks[5], (D_MODEL,), dtype=jnp.float32) * 0.01, 'ln_gamma': jnp.ones((D_MODEL,), dtype=jnp.float32), 'ln_beta': jnp.zeros((D_MODEL,), dtype=jnp.float32)}
    _L0_xattn_all = _L0_xattn_setup()
    _L0_xattn_in = {k: v for k, v in _L0_xattn_all.items() if k in ('W_qkv', 'b_qkv', 'W_o', 'b_o', 'ln_gamma', 'ln_beta')}
    del _L0_xattn_all

    def _L1_xattn_setup():
        import jax, jax.numpy as jnp
        import numpy as np
        D_MODEL = 512
        NUM_HEADS = 16
        HEAD_DIM = D_MODEL // NUM_HEADS
        LN_EPS = 1e-05

        def _split_heads(x):
            B, S, _ = x.shape
            return x.reshape(B, S, NUM_HEADS, HEAD_DIM).transpose(0, 2, 1, 3)
        key = jax.random.key(seed)
        ks = jax.random.split(key, 12)
        B, SQ, SKV = (4, 1024, 1024)
        s = 1.0 / np.sqrt(D_MODEL)
        inp = {'query': jax.random.normal(ks[0], (B, SQ, D_MODEL), jnp.float32), 'key_value': jax.random.normal(ks[1], (B, SKV, D_MODEL), jnp.float32), 'Wq': jax.random.normal(ks[2], (D_MODEL, D_MODEL), jnp.float32) * s, 'bq': jnp.zeros((D_MODEL,), jnp.float32), 'Wk': jax.random.normal(ks[3], (D_MODEL, D_MODEL), jnp.float32) * s, 'bk': jnp.zeros((D_MODEL,), jnp.float32), 'Wv': jax.random.normal(ks[4], (D_MODEL, D_MODEL), jnp.float32) * s, 'bv': jnp.zeros((D_MODEL,), jnp.float32), 'Wo': jax.random.normal(ks[5], (D_MODEL, D_MODEL), jnp.float32) * s, 'bo': jnp.zeros((D_MODEL,), jnp.float32), 'gamma': jnp.ones((D_MODEL,), jnp.float32), 'beta': jnp.zeros((D_MODEL,), jnp.float32)}
        return inp
    _L1_xattn_all = _L1_xattn_setup()
    _L1_xattn_in = {k: v for k, v in _L1_xattn_all.items() if k in ('Wq', 'bq', 'Wk', 'bk', 'Wv', 'bv', 'Wo', 'bo', 'gamma', 'beta')}
    del _L1_xattn_all
    return {'x': x, 'ctx_1024': ctx_1024, 'L0_xattn_W_qkv': _L0_xattn_in['W_qkv'], 'L0_xattn_b_qkv': _L0_xattn_in['b_qkv'], 'L0_xattn_W_o': _L0_xattn_in['W_o'], 'L0_xattn_b_o': _L0_xattn_in['b_o'], 'L0_xattn_ln_gamma': _L0_xattn_in['ln_gamma'], 'L0_xattn_ln_beta': _L0_xattn_in['ln_beta'], 'L1_xattn_Wq': _L1_xattn_in['Wq'], 'L1_xattn_bq': _L1_xattn_in['bq'], 'L1_xattn_Wk': _L1_xattn_in['Wk'], 'L1_xattn_bk': _L1_xattn_in['bk'], 'L1_xattn_Wv': _L1_xattn_in['Wv'], 'L1_xattn_bv': _L1_xattn_in['bv'], 'L1_xattn_Wo': _L1_xattn_in['Wo'], 'L1_xattn_bo': _L1_xattn_in['bo'], 'L1_xattn_gamma': _L1_xattn_in['gamma'], 'L1_xattn_beta': _L1_xattn_in['beta']}

def reference(x, ctx_1024, L0_xattn_W_qkv, L0_xattn_b_qkv, L0_xattn_W_o, L0_xattn_b_o, L0_xattn_ln_gamma, L0_xattn_ln_beta, L1_xattn_Wq, L1_xattn_bq, L1_xattn_Wk, L1_xattn_bk, L1_xattn_Wv, L1_xattn_bv, L1_xattn_Wo, L1_xattn_bo, L1_xattn_gamma, L1_xattn_beta):
    import jax
    import jax.numpy as jnp

    def _L0_xattn_ref(query, key_value, W_qkv, b_qkv, W_o, b_o, ln_gamma, ln_beta):
        import jax, jax.numpy as jnp
        import numpy as np
        D_MODEL = 512
        N_HEADS = 16
        D_K = D_MODEL // N_HEADS
        LN_EPS = 1e-05

        def _attention(query, key_value, W_qkv, b_qkv, W_o, b_o, ln_gamma, ln_beta):
            B, Sq, _ = query.shape
            Skv = key_value.shape[1]
            Wq, Wk, Wv = (W_qkv[:D_MODEL], W_qkv[D_MODEL:2 * D_MODEL], W_qkv[2 * D_MODEL:])
            bq, bk, bv = (b_qkv[:D_MODEL], b_qkv[D_MODEL:2 * D_MODEL], b_qkv[2 * D_MODEL:])
            Q = (query @ Wq.T + bq).reshape(B, Sq, N_HEADS, D_K).transpose(0, 2, 1, 3)
            K = (key_value @ Wk.T + bk).reshape(B, Skv, N_HEADS, D_K).transpose(0, 2, 1, 3)
            V = (key_value @ Wv.T + bv).reshape(B, Skv, N_HEADS, D_K).transpose(0, 2, 1, 3)
            scores = jnp.einsum('bhqd,bhkd->bhqk', Q.astype(jnp.float32), K.astype(jnp.float32))
            scores = scores / np.sqrt(D_K)
            attn = jax.nn.softmax(scores, axis=-1)
            context = jnp.einsum('bhqk,bhkd->bhqd', attn, V.astype(jnp.float32)).astype(query.dtype)
            context = context.transpose(0, 2, 1, 3).reshape(B, Sq, D_MODEL)
            output = context @ W_o.T + b_o
            x = output + query
            mu = jnp.mean(x, axis=-1, keepdims=True)
            var = jnp.mean(jnp.square(x - mu), axis=-1, keepdims=True)
            return (x - mu) / jnp.sqrt(var + LN_EPS) * ln_gamma + ln_beta
        return _attention(query, key_value, W_qkv, b_qkv, W_o, b_o, ln_gamma, ln_beta)

    def _L1_xattn_ref(query, key_value, Wq, bq, Wk, bk, Wv, bv, Wo, bo, gamma, beta):
        import jax, jax.numpy as jnp
        import numpy as np
        D_MODEL = 512
        NUM_HEADS = 16
        HEAD_DIM = D_MODEL // NUM_HEADS
        LN_EPS = 1e-05

        def _split_heads(x):
            B, S, _ = x.shape
            return x.reshape(B, S, NUM_HEADS, HEAD_DIM).transpose(0, 2, 1, 3)
        B, SQ, D = query.shape
        Q = _split_heads(query @ Wq.T + bq)
        K = _split_heads(key_value @ Wk.T + bk)
        V = _split_heads(key_value @ Wv.T + bv)
        scale = 1.0 / np.sqrt(HEAD_DIM).astype(np.float32)
        scores = jnp.einsum('bhqd,bhkd->bhqk', Q, K) * scale
        attn = jax.nn.softmax(scores, axis=-1)
        ctx = jnp.einsum('bhqk,bhkd->bhqd', attn, V)
        ctx = ctx.transpose(0, 2, 1, 3).reshape(B, SQ, D)
        out = ctx @ Wo.T + bo
        x = query + out
        mu = jnp.mean(x, axis=-1, keepdims=True)
        var = jnp.mean(jnp.square(x - mu), axis=-1, keepdims=True)
        return (x - mu) * jax.lax.rsqrt(var + LN_EPS) * gamma + beta
    x = _L0_xattn_ref(x, ctx_1024, L0_xattn_W_qkv, L0_xattn_b_qkv, L0_xattn_W_o, L0_xattn_b_o, L0_xattn_ln_gamma, L0_xattn_ln_beta)
    x = _L1_xattn_ref(x, ctx_1024, L1_xattn_Wq, L1_xattn_bq, L1_xattn_Wk, L1_xattn_bk, L1_xattn_Wv, L1_xattn_bv, L1_xattn_Wo, L1_xattn_bo, L1_xattn_gamma, L1_xattn_beta)
    return x

_drawn_inputs = setup_inputs


def setup_inputs(seed=0):
    import zlib

    import numpy as np

    out = dict(_drawn_inputs(seed))
    spreads = {'L0_xattn_ln_gamma': (1.0, 0.2),
     'L0_xattn_ln_beta': (0.0, 0.1),
     'L1_xattn_bq': (0.0, 0.464),
     'L1_xattn_bk': (0.0, 0.8),
     'L1_xattn_bv': (0.0, 0.1),
     'L1_xattn_bo': (0.0, 0.1),
     'L1_xattn_gamma': (1.0, 0.2),
     'L1_xattn_beta': (0.0, 0.1)}
    factors = {'L0_xattn_b_qkv': 7.237, 'L0_xattn_b_o': 7.022}
    for name, (base, spread) in spreads.items():
        noise = np.random.default_rng([zlib.crc32(name.encode()), seed]).standard_normal(out[name].shape)
        drawn = base * np.exp(spread * noise) if base else spread * noise
        out[name] = jnp.asarray(drawn.astype(out[name].dtype))
    for name, factor in factors.items():
        out[name] = (out[name] * factor).astype(out[name].dtype)
    return out
```

```python
from contextlib import ExitStack

import concourse.bass as bass
from concourse import mybir

F32 = mybir.dt.float32
F32R = mybir.dt.float32r
ALU = mybir.AluOpType
ACT = mybir.ActivationFunctionType
AX = mybir.AxisListType

LAYERS = 2
HEADS = 16
GROUP = 4
UNITS = HEADS // GROUP
LN_EPS = 1e-5

PROJ_USES = ["K0", "K1", "Q", "V0", "M0", "V1", "V2", "O0", "O1", "T0", "T1", "M1"]
STEPS = ["S0", "S1", "K0", "S2", "K1", "S3", "Q", "S4", "V0", "M0", "S5", "V1", "S6", "V2", "S7", "O0", "O1", "T0", "T1"]
AHEAD = 4


def wait(engine, semaphore, count):
    if not isinstance(count, int) or count > 0:
        engine.wait_ge(semaphore, count)


def cross_attention_stack(nc, x, x_t, ctx_t, w_pieces, bias_cols, bias_rows, identity, out):
    B, SQ, D = x.shape
    P = 128
    KT = D // P
    SKV = ctx_t.shape[3]
    DK = D // HEADS
    KEYS = 125
    NKT = SKV // KEYS
    QH = SQ // 2
    SPAN = 376
    K_HALVES = [(0, SPAN), (SPAN, SKV)]
    ITEMS = LAYERS * B
    PAIRS = GROUP * NKT // 2
    PER_HEAD = NKT // 2
    PAIR = 2 * SQ
    SCALE = float(DK) ** -0.5
    VCOLS = 2 * DK + 1
    PIECE = 512
    assert D == KT * P and SKV == NKT * KEYS and DK * GROUP == P and PAIR <= 512 and 2 * SPAN >= SKV

    LO_ON_DVE = [c % 3 == 2 for c in range(PAIRS)]
    N_LO_DVE = sum(LO_ON_DVE)
    N_LO_POOL = PAIRS - N_LO_DVE

    FIRST = [("k", 0), ("c", 0), ("c", 1), ("c", 2), ("c", 3), ("q", 0), ("x", 0), ("x", 1), ("v", 0), ("v", 1),
             ("k", 1), ("q", 1), ("k", 2), ("q", 2), ("v", 2), ("v", 3), ("k", 3), ("q", 3),
             ("o", 0), ("o", 1), ("o", 2), ("o", 3)]
    ITEM_PIECES = [("c", 0), ("c", 1), ("c", 2), ("c", 3), ("x", 0), ("x", 1)]
    REFRESH = {0: [("k", 0), ("q", 0)], 1: [("k", 1), ("q", 1), ("v", 0), ("v", 1)],
               2: [("k", 2), ("q", 2)], 3: [("k", 3), ("q", 3), ("v", 2), ("v", 3)]}
    NP_ITEM = len(ITEM_PIECES)
    NP_REFRESH = sum(len(p) for p in REFRESH.values())
    PIECE_INDEX = {**{("k", g): g for g in range(4)}, **{("q", g): 4 + g for g in range(4)},
                   **{("v", n): 8 + n for n in range(4)}, **{("o", k): 12 + k for k in range(4)}}

    x1 = nc.dram_tensor("x1", (B, SQ, D), F32, kind="Internal").ap()
    x1_t = nc.dram_tensor("x1_t", (B, P, KT, SQ), F32, kind="Internal").ap()

    class Item:

        def __init__(self, i, lo, pj0, raw0):
            self.i, self.lo = i, lo
            self.layer = 0 if lo < B else 1
            self.first = lo == 0
            self.tail = lo == ITEMS
            self.refresh = lo == B - 1
            self.refresh_out = lo == B
            self.out_layer = 0 if lo <= B else 1
            self.pj0, self.raw0 = pj0, raw0

        def attends(self, g):
            return not (self.first and g == 0) and not (self.tail and g > 0)

        def does(self, g, step):
            if step[0] in "KQV":
                return not self.tail
            if step[0] in "SM":
                return self.attends(g)
            if step[0] == "O":
                return not self.first and g == 1
            return not self.first and self.out_layer == 0 and g == 2 + int(step[1])

        def groups(self, g):
            return [name for name in PROJ_USES if self.does(g, name)]

        def n_groups(self):
            return sum(len(self.groups(g)) for g in range(UNITS))

        def pj(self, g, name):
            n = sum(len(self.groups(h)) for h in range(g)) + self.groups(g).index(name)
            return n % 2, self.pj0 + n // 2

        def n_raw(self):
            return NP_REFRESH * self.refresh + 4 * self.refresh_out + NP_ITEM * (self.lo < ITEMS - 1)

        def raw(self, n):
            return n % 2, self.raw0 + n // 2

    SEGMENTS = [(0, 1), (1, B - 1), (B - 1, B), (B, B + 1), (B + 1, ITEMS - 1), (ITEMS - 1, ITEMS), (ITEMS, ITEMS + 1)]

    def items(engine):
        pj0, raw0 = 0, len(FIRST) // 2
        for lo, hi in SEGMENTS:
            probe = Item(lo, lo, 0, 0)
            assert probe.n_groups() % 2 == 0 and probe.n_raw() % 2 == 0
            n_pj, n_raw = probe.n_groups() // 2, probe.n_raw() // 2
            if hi - lo == 1:
                yield Item(lo, lo, pj0, raw0)
            else:
                with engine.Fori(lo, hi) as i:
                    yield Item(i, lo, i * n_pj + (pj0 - lo * n_pj), i * n_raw + (raw0 - lo * n_raw))
            pj0 += n_pj * (hi - lo)
            raw0 += n_raw * (hi - lo)

    def item_raw_at(it):
        return NP_REFRESH * it.refresh + 4 * it.refresh_out

    with ExitStack() as stack:
        def sb(name, shape, dt=F32):
            return stack.enter_context(nc.sbuf_tensor(name, shape, dt))

        def psum(name, shape):
            return stack.enter_context(nc.psum_tensor(name, shape, F32))

        def sem(name):
            return stack.enter_context(nc.semaphore(name))

        w_hi = sb("w_hi", [P, 4, KT, D], F32R)
        w_lo = sb("w_lo", [P, 4, KT, D], F32R)
        c_hi = sb("c_hi", [P, KT, SKV], F32R)
        c_lo = sb("c_lo", [P, KT, SKV], F32R)
        x_hi = sb("x_hi", [P, KT, SQ], F32R)
        x_lo = sb("x_lo", [P, KT, SQ], F32R)
        raw = sb("raw", [P, 2, SKV])
        k_stack = sb("k_stack", [P, 2, GROUP, SKV], F32R)
        q_stack = sb("q_stack", [P, 2, GROUP, SQ], F32R)
        v_sb = sb("v_sb", [KEYS, 2, NKT, 2 * GROUP, VCOLS], F32R)
        e_ring = sb("e_ring", [KEYS, 3, PAIR])
        e_hi = sb("e_hi", [P, 4, PAIR], F32R)
        e_lo = sb("e_lo", [P, 4, PAIR], F32R)
        k_stage = [t[:, 0:2, :].rearrange("p a n -> p (a n)")[:, 0:SKV] for t in (e_hi, e_lo)]
        q_stage = [t[:, 2, 0:SQ] for t in (e_hi, e_lo)]
        row_max = sb("row_max", [P, 2, 2, 2])
        pv_sb = sb("pv_sb", [VCOLS, 2, PAIR])
        pv_wide = sb("pv_wide", [P, 3, SQ])
        a_hi = sb("a_hi", [P, UNITS, SQ], F32R)
        a_lo = sb("a_lo", [P, UNITS, SQ], F32R)
        y_sb = sb("y_sb", [P, 2, D])
        yt_sb = sb("yt_sb", [P, KT, QH])
        cols = sb("cols", [P, LAYERS, 3, UNITS])
        rows = sb("rows", [P, 3, D])
        ident = sb("ident", [P, P])
        eps = sb("eps", [P, 1])
        stats = sb("stats", [P, 2, 6])
        moments = sb("moments", [P, 2, 2])
        rstd = sb("rstd", [P, 6, 2])

        proj = psum("proj", [P, 2, 512])
        sc = psum("sc", [P, 4, 512])
        pv = psum("pv", [P, 2, 512])

        consts_loaded = sem("consts_loaded")
        rows_loaded = sem("rows_loaded")
        raw_loaded = [sem(f"raw_loaded{n}") for n in range(2)]
        raw_hi = [sem(f"raw_hi{n}") for n in range(2)]
        raw_split = [sem(f"raw_split{n}") for n in range(2)]
        zeroed = sem("zeroed")
        selectors_loaded = sem("selectors_loaded")
        proj_ready = [sem(f"proj_ready{n}") for n in range(2)]
        hi_done = sem("hi_done")
        proj_taken = [sem(f"proj_taken{n}") for n in range(2)]
        stack_loaded = [sem(f"stack_loaded{n}") for n in range(2)]
        scores_ready = sem("scores_ready")
        max_done = sem("max_done")
        shifted_ready = sem("shifted_ready")
        exp_done = sem("exp_done")
        e_hi_done = sem("e_hi_done")
        e_lo_dve = sem("e_lo_dve")
        e_lo_pool = sem("e_lo_pool")
        pv_done = sem("pv_done")
        pv_taken = sem("pv_taken")
        wide_loaded = sem("wide_loaded")
        norm_step = sem("norm_step")
        y_loaded = sem("y_loaded")
        y_biased = sem("y_biased")
        ln_step = sem("ln_step")
        ln_act = sem("ln_act")
        stats_seen = sem("stats_seen")
        normed = sem("normed")
        pool_step = sem("pool_step")
        out_ready = sem("out_ready")
        out_stored = sem("out_stored")
        yt_stored = sem("yt_stored")

        block = stack.enter_context(nc.Block())

        STACK_DMAS = 6
        WIDE_DMAS = 6
        NORM_STEPS = 5
        LN_STEPS = 10
        f32 = lambda ap: ap.bitcast(F32)

        def piece_columns(kind, n):
            return {"c": SKV, "x": 2 * SQ}.get(kind, PIECE)

        def piece_source(kind, n, item, layer):
            if kind == "c":
                return ctx_t[item - B if layer else item, :, n, :]
            if kind == "x":
                return (x1_t[item - B] if layer else x_t[item])[:, 2 * n:2 * n + 2, :]
            return w_pieces[layer, PIECE_INDEX[kind, n]]

        def piece_targets(kind, n):
            if kind == "c":
                return [t[:, n, :] for t in (c_hi, c_lo)]
            if kind == "x":
                return [t[:, 2 * n:2 * n + 2, :] for t in (x_hi, x_lo)]
            if kind in "kq":
                return [t[:, "kq".index(kind), :, n * P:(n + 1) * P] for t in (w_hi, w_lo)]
            if kind == "v":
                half, k = divmod(n, 2)
                return [t[:, 2, 2 * k:2 * k + 2, half * 2 * P:(half + 1) * 2 * P] for t in (w_hi, w_lo)]
            return [t[:, 3, n, :] for t in (w_hi, w_lo)]

        def piece_raw(kind, n, slot):
            flat = raw[:, slot, 0:piece_columns(kind, n)]
            if kind == "c" or kind == "o":
                return flat
            return flat.rearrange("p (a n) -> p a n", a=4 if kind in "kq" else 2)

        def pieces_of(it, g):
            found = []
            if it.refresh:
                at = sum(len(REFRESH[h]) for h in range(g))
                found += [(at + m, *p) for m, p in enumerate(REFRESH[g])]
            if it.refresh_out and g == 1:
                found += [(m, "o", m) for m in range(4)]
            if g == 3 and it.lo < ITEMS - 1:
                found += [(item_raw_at(it) + m, *p) for m, p in enumerate(ITEM_PIECES)]
            return found

        def readers_done(it, g, kind, engine):
            bank, k = it.pj(g, "O1" if kind == "o" else "V2")
            engine.wait_ge(proj_ready[bank], k + 1)

        def stack_wait(engine, it, g):
            if not it.tail:
                engine.wait_ge(stack_loaded[g % 2], (it.i * 2 + g // 2 + 1) * (16 * STACK_DMAS))

        def lo_done(engine, v, c):
            v, c = (v, c) if c >= 0 else (v - 1, c + PAIRS)
            n = sum(LO_ON_DVE[:c + 1])
            if LO_ON_DVE[c]:
                wait(engine, e_lo_dve, v * N_LO_DVE + n)
            else:
                wait(engine, e_lo_pool, v * N_LO_POOL + c + 1 - n)

        @block.sync
        def _(sp):
            sp.dma_start(cols[:, :, :, :], bias_cols).then_inc(consts_loaded, 16)
            sp.dma_start(ident[:, :], identity).then_inc(consts_loaded, 16)
            sp.dma_start(rows[:, :, :], bias_rows[0]).then_inc(rows_loaded, 16)

            def load_raw(slot, free, kind, m, item, layer):
                wait(sp, raw_split[slot], free)
                sp.dma_start(piece_raw(kind, m, slot), piece_source(kind, m, item, layer)).then_inc(raw_loaded[slot], 16)

            for n, (kind, m) in enumerate(FIRST):
                load_raw(n % 2, n // 2, kind, m, 0, 0)
            sp.wait_ge(zeroed, 3)
            for b in range(2):
                for j in range(GROUP):
                    r = 3 * DK + j % 2
                    sp.dma_start(f32(k_stack[r:r + 1, b, j, :]), f32(k_stage[0][0:1, :])).then_inc(selectors_loaded, 16)

            for it in items(sp):
                value = (lambda v: v) if isinstance(it.i, int) else sp.snap
                if not it.tail:
                    taken = {(g, name): value(it.pj(g, name)[1] + 1) for g in range(UNITS) for name in ("K1", "Q")}
                    free = [value(it.raw(n)[1]) for n in range(it.n_raw())]
                pv_count = [value(it.i * (2 * UNITS) + 2 * g) for g in range(UNITS)]
                twice = value(it.i * 2)
                turned = {g: value(it.pj(g, f"T{g - 2}")[1] + 1) for g in (2, 3) if it.does(g, f"T{g - 2}")}
                stored = value(it.i * 32)
                for g in range(UNITS):
                    b = g % 2
                    if not it.tail:
                        sp.wait_ge(proj_taken[it.pj(g, "K1")[0]], taken[g, "K1"])
                        for r, part in ((0, 0), (DK, 0), (2 * DK, 1)):
                            sp.dma_start(f32(k_stack[r:r + DK, b, :, :]), f32(k_stage[part])).then_inc(stack_loaded[b], 16)
                        sp.wait_ge(proj_taken[it.pj(g, "Q")[0]], taken[g, "Q"])
                        for r, part in ((0, 0), (DK, 1), (2 * DK, 0)):
                            sp.dma_start(f32(q_stack[r:r + DK, b, :, :]), f32(q_stage[part])).then_inc(stack_loaded[b], 16)
                    for n, kind, m in pieces_of(it, g):
                        load_raw(it.raw(n)[0], free[n], kind, m, it.i + 1, 1 if kind not in "cx" or it.lo >= B - 1 else 0)
                    if it.attends(g):
                        sp.wait_ge(pv_taken, pv_count[g])
                        for part in range(2):
                            src = pv_sb[part * DK:(part + 1) * DK, :, :].rearrange("d a (b q) -> d (a b) q", b=2)
                            sp.dma_start(pv_wide[:, part, :], src).then_inc(wide_loaded, 16)
                        for j in range(GROUP):
                            one = pv_sb[2 * DK:2 * DK + 1, :, :]
                            src = bass.AP(one.tensor, one.offset + j * SQ, [[2 * PAIR, 1], [0, DK], [1, SQ]])
                            sp.dma_start(pv_wide[j:P:GROUP, 2, :], src).then_inc(wide_loaded, 16)
                    if not it.first and g == 1:
                        sp.wait_ge(out_ready, twice)
                        dst = out[it.i - 1 - B] if it.out_layer else x1[it.i - 1]
                        for t in range(2):
                            sp.dma_start(dst[t * QH:(t + 1) * QH, :], y_sb[0:QH, t, :]).then_inc(out_stored, 16)
                        if it.refresh_out:
                            sp.dma_start(rows[:, :, :], bias_rows[1]).then_inc(rows_loaded, 16)
                    if g in turned:
                        t = g - 2
                        sp.wait_ge(proj_taken[it.pj(g, f"T{t}")[0]], turned[g])
                        sp.dma_start(x1_t[it.i - 1, :, :, t * QH:(t + 1) * QH], yt_sb[:, :, :]).then_inc(yt_stored, 16)
                    if g == 3 and not it.tail:
                        wait(sp, out_stored, stored)
                        if it.out_layer == 0:
                            wait(sp, yt_stored, stored)
                        src = x1[it.i - B] if it.layer else x[it.i]
                        sp.dma_start(y_sb[0:QH, :, :], src.rearrange("(t q) d -> q t d", q=QH)).then_inc(y_loaded, 16)
            sp.wait_ge(out_stored, 32 * ITEMS)
            sp.wait_ge(yt_stored, 32 * B)

        @block.tensor
        def _(pe):
            def free_bank(it, g, name):
                bank, k = it.pj(g, name)
                wait(pe, proj_taken[bank], k)
                return bank

            def three_passes(target, w, w2, a, a2, k):
                nc.tensor.matmul(target, w, a, start=(k == 0), stop=False)
                nc.tensor.matmul(target, w2, a, start=False, stop=False)
                return nc.tensor.matmul(target, w, a2, start=False, stop=(k == KT - 1))

            def first_split(it, n):
                if it.first:
                    pe.wait_ge(raw_split[n % 2], n // 2 + 1)
                    pe.wait_ge(raw_split[1 - n % 2], (n + 1) // 2)

            def project_keys(it, g, half):
                first_split(it, [4, 10, 12, 16][g])
                if not it.first and g == 0 and half == 0:
                    for slot in range(2):
                        pe.wait_ge(raw_split[slot], it.raw0)
                lo, hi = K_HALVES[half]
                bank = free_bank(it, g, f"K{half}")
                for k in range(KT):
                    cs = slice(g * P, (g + 1) * P)
                    mm = three_passes(proj[:, bank, 0:hi - lo], w_hi[:, 0, k, cs], w_lo[:, 0, k, cs],
                                      c_hi[:, k, lo:hi], c_lo[:, k, lo:hi], k)
                mm.then_inc(proj_ready[bank], 1)

            def project_queries(it, g):
                first_split(it, [7, 11, 13, 17][g])
                bank = free_bank(it, g, "Q")
                for k in range(KT):
                    cs = slice(g * P, (g + 1) * P)
                    mm = three_passes(proj[:, bank, 0:SQ], w_hi[:, 1, k, cs], w_lo[:, 1, k, cs],
                                      x_hi[:, k, :], x_lo[:, k, :], k)
                mm.then_inc(proj_ready[bank], 1)

            def project_values(it, g, n):
                first_split(it, [9, 9, 15, 15][g])
                half, kt = g // 2, 3 * (g % 2) + n
                bank = free_bank(it, g, f"V{n}")
                ks = slice(kt * KEYS, (kt + 1) * KEYS)
                ds = slice(half * 2 * P, (half + 1) * 2 * P)
                for k in range(KT):
                    mm = three_passes(proj[0:KEYS, bank, 0:2 * P], c_hi[:, k, ks], c_lo[:, k, ks],
                                      w_hi[:, 2, k, ds], w_lo[:, 2, k, ds], k)
                mm.then_inc(proj_ready[bank], 1)

            def scores(v, t, b):
                j, qt = divmod(t, 2)
                if t < 2:
                    wait(pe, exp_done, v * PAIRS - (2 if t == 0 else 0))
                else:
                    pe.wait_ge(max_done, v * (2 * GROUP) + (t - 1))
                q = q_stack[0:3 * DK, b, j, qt * QH:(qt + 1) * QH]
                at = 2 * (t % 2)
                nc.tensor.matmul(sc[0:QH, at, 0:SPAN], q, k_stack[0:3 * DK, b, j, 0:SPAN], start=True, stop=True)
                nc.tensor.matmul(sc[0:QH, at + 1, 0:SPAN], q, k_stack[0:3 * DK, b, j, SKV - SPAN:SKV],
                                 start=True, stop=True).then_inc(scores_ready, 1)

            def turn_maxima(it, g, v, pair):
                bank = free_bank(it, g, f"M{pair}")
                pe.wait_ge(max_done, v * (2 * GROUP) + 4 * (pair + 1))
                for qt in range(2):
                    mm = nc.tensor.transpose(proj[0:2, bank, qt * QH:(qt + 1) * QH], row_max[0:QH, pair, qt, :],
                                             ident[0:QH, 0:QH])
                mm.then_inc(proj_ready[bank], 1)

            def shifted_scores(it, g, v, c, b):
                j, m = divmod(c, PER_HEAD)
                if c in (0, 2 * PER_HEAD):
                    bank, k = it.pj(g, f"M{c // (2 * PER_HEAD)}")
                    pe.wait_ge(proj_taken[bank], k + 1)
                if c in (0, 2):
                    pe.wait_ge(max_done, v * (2 * GROUP) + (2 * GROUP - 1 + c // 2))
                if c >= 4:
                    pe.wait_ge(exp_done, v * PAIRS + (c - 3))
                for n in range(2):
                    ks = slice((2 * m + n) * KEYS, (2 * m + n + 1) * KEYS)
                    mm = nc.tensor.matmul(sc[0:KEYS, c % 4, n * SQ:(n + 1) * SQ], k_stack[:, b, j, ks], q_stack[:, b, j, :],
                                          start=True, stop=True)
                mm.then_inc(shifted_ready, 1)

            def times_values(v, c, gv):
                j, m = divmod(c, PER_HEAD)
                if c in (0, 2 * PER_HEAD):
                    wait(pe, pv_taken, v * 2 - 1 + c // (2 * PER_HEAD))
                pe.wait_ge(e_hi_done, v * PAIRS + (c + 1))
                lo_done(pe, v, c)
                for n in range(2):
                    kt = 2 * m + n
                    target = pv[0:VCOLS, j // 2, (j % 2) * SQ:(j % 2 + 1) * SQ]
                    values = v_sb[:, gv // 2, kt, GROUP * (gv % 2) + j, :]
                    nc.tensor.matmul(target, values, e_hi[0:KEYS, c % 4, n * SQ:(n + 1) * SQ], start=(kt == 0), stop=False)
                    mm = nc.tensor.matmul(target, values, e_lo[0:KEYS, c % 4, n * SQ:(n + 1) * SQ],
                                          start=False, stop=(kt == NKT - 1))
                mm.then_inc(pv_done, 1)

            def project_out(it, g, t):
                bank = free_bank(it, g, f"O{t}")
                pe.wait_ge(norm_step, it.i * (UNITS * NORM_STEPS))
                qs = slice(t * QH, (t + 1) * QH)
                for k in range(KT):
                    mm = three_passes(proj[0:QH, bank, 0:D], a_hi[:, k, qs], a_lo[:, k, qs],
                                      w_hi[:, 3, k, :], w_lo[:, 3, k, :], k)
                mm.then_inc(proj_ready[bank], 1)

            def turn_output(it, g, t):
                bank = free_bank(it, g, f"T{t}")
                pe.wait_ge(out_ready, it.i * 2 - 1 + t)
                for k in range(KT):
                    mm = nc.tensor.transpose(proj[:, bank, k * QH:(k + 1) * QH], y_sb[0:QH, t, k * P:(k + 1) * P],
                                             ident[0:QH, 0:QH])
                mm.then_inc(proj_ready[bank], 1)

            pe.wait_ge(consts_loaded, 32)
            pe.wait_ge(zeroed, 5)
            pe.wait_ge(selectors_loaded, 16 * 2 * GROUP)
            for it in items(pe):
                for g in range(UNITS):
                    v = it.i * UNITS + (g - 1)
                    b = (g + 1) % 2
                    if it.attends(g):
                        pe.wait_ge(stack_loaded[b], (it.i * 2 + ((g - 1) // 2 + 1)) * (16 * STACK_DMAS))
                    for step in STEPS:
                        if not it.does(g, step):
                            continue
                        n = int(step[1:] or 0)
                        if step[0] == "S":
                            scores(v, n, b)
                        elif step[0] == "M":
                            turn_maxima(it, g, v, n)
                        elif step[0] == "K":
                            project_keys(it, g, n)
                        elif step[0] == "Q":
                            project_queries(it, g)
                        elif step[0] == "V":
                            project_values(it, g, n)
                        elif step[0] == "O":
                            project_out(it, g, n)
                        else:
                            turn_output(it, g, n)
                    if it.attends(g):
                        for c in range(PAIRS + AHEAD):
                            if c < PAIRS:
                                shifted_scores(it, g, v, c, b)
                            if c == AHEAD - 1:
                                turn_maxima(it, g, v, 1)
                            if c == AHEAD and not it.tail:
                                bank, k = it.pj(g, "V2")
                                pe.wait_ge(proj_taken[bank], k + 1)
                            if c >= AHEAD:
                                times_values(v, c - AHEAD, (g - 1) % UNITS)

        @block.scalar
        def _(act):
            act.preload_act_table_set("natural_log_exp_and_others")

            def split_hi(slot, k, kind, m):
                act.wait_ge(raw_loaded[slot], (k + 1) * 16)
                nc.scalar.activation(piece_targets(kind, m)[0], piece_raw(kind, m, slot), ACT.Copy).then_inc(raw_hi[slot], 1)

            def split_piece(it, g, piece):
                n, kind, m = piece
                readers_done(it, g, kind, act)
                split_hi(*it.raw(n), kind, m)

            def evacuate(it, g, name):
                bank, k = it.pj(g, name)
                act.wait_ge(proj_ready[bank], k + 1)
                if name[0] == "V":
                    half, kt = g // 2, 3 * (g % 2) + int(name[1])
                    nc.scalar.activation(v_sb[:, half, kt, :, 0:DK], proj[0:KEYS, bank, 0:2 * P].rearrange("p (h d) -> p h d", d=DK),
                                         ACT.Copy).then_inc(hi_done, 1)
                elif name == "Q":
                    nc.scalar.activation(q_stage[0], proj[:, bank, 0:SQ], ACT.Identity,
                                         bias=cols[:, it.layer, 1, g:g + 1]).then_inc(hi_done, 1)
                else:
                    lo, hi = K_HALVES[int(name[1])]
                    nc.scalar.activation(k_stage[0][:, lo:hi], proj[:, bank, 0:hi - lo], ACT.Identity,
                                         bias=cols[:, it.layer, 0, g:g + 1]).then_inc(hi_done, 1)

            def maxima_rows(it, g, pair, b):
                bank, k = it.pj(g, f"M{pair}")
                act.wait_ge(proj_ready[bank], k + 1)
                turned = proj[0:2, bank, 0:SQ].unsqueeze(1).broadcast_to([2, 2, SQ])
                nc.scalar.activation(q_stack[3 * DK:3 * DK + 2, b, 2 * pair:2 * pair + 2, :], turned, ACT.Copy,
                                     scale=-1.0).then_inc(proj_taken[bank], 1)

            def take_products(v, n):
                act.wait_ge(pv_done, v * PAIRS + 2 * PER_HEAD * (n + 1))
                wait(act, wide_loaded, v * (16 * WIDE_DMAS))
                nc.scalar.activation(pv_sb[:, n, :], pv[0:VCOLS, n, 0:PAIR], ACT.Copy).then_inc(pv_taken, 1)

            def deviation(it):
                act.wait_ge(ln_step, it.i * LN_STEPS - (LN_STEPS - 4))
                nc.scalar.activation(rstd[0:QH, 0, :], moments[0:QH, :, 1], ACT.Ln, bias=eps[0:QH, :]).then_inc(ln_act, 1)
                act.wait_ge(ln_act, it.i * 2 - 1)
                nc.scalar.activation(rstd[0:QH, 1, :], rstd[0:QH, 0, :], ACT.Exp, scale=-0.5).then_inc(ln_act, 1)

            for n, (kind, m) in enumerate(FIRST):
                split_hi(n % 2, n // 2, kind, m)
            act.wait_ge(consts_loaded, 32)
            act.wait_ge(zeroed, 5)
            act.wait_ge(selectors_loaded, 16 * 2 * GROUP)
            for it in items(act):
                for g in range(UNITS):
                    v = it.i * UNITS + (g - 1)
                    b = (g + 1) % 2
                    for name in STEPS:
                        if name[0] in "SO" or not it.does(g, name):
                            continue
                        if name == "M0":
                            maxima_rows(it, g, 0, b)
                        elif name[0] == "T":
                            bank, k = it.pj(g, name)
                            act.wait_ge(proj_ready[bank], k + 1)
                            if name == "T1":
                                act.wait_ge(yt_stored, it.i * 32 - 16)
                            nc.scalar.activation(yt_sb[:, :, :], proj[:, bank, 0:KT * QH].rearrange("p (k q) -> p k q", q=QH),
                                                 ACT.Copy).then_inc(proj_taken[bank], 1)
                        else:
                            evacuate(it, g, name)
                    if it.attends(g):
                        pieces = pieces_of(it, g)
                        for c in range(PAIRS):
                            act.wait_ge(shifted_ready, v * PAIRS + (c + 1))
                            wait(act, e_hi_done, v * PAIRS + (c - 2))
                            lo_done(act, v, c - 3)
                            nc.scalar.activation(e_ring[:, c % 3, :], sc[0:KEYS, c % 4, 0:PAIR], ACT.Exp,
                                                 scale=SCALE).then_inc(exp_done, 1)
                            if c == 0:
                                maxima_rows(it, g, 1, b)
                            if c == 3 and g == 1 and not it.first:
                                deviation(it)
                            if c == 9:
                                take_products(v, 0)
                            if c % 2 == 1 and pieces:
                                split_piece(it, g, pieces.pop(0))
                        for piece in pieces:
                            split_piece(it, g, piece)
                        take_products(v, 1)
                    elif it.tail and g == 1:
                        deviation(it)

        @block.vector
        def _(dve):
            def split_lo(slot, k, kind, m):
                dve.wait_ge(raw_hi[slot], k + 1)
                hi, lo = piece_targets(kind, m)
                nc.vector.tensor_tensor(lo, piece_raw(kind, m, slot), f32(hi), ALU.subtract).then_inc(raw_split[slot], 1)

            def row_maxima(v, t):
                j, qt = divmod(t, 2)
                at = 2 * (t % 2)
                dve.wait_ge(scores_ready, v * (2 * GROUP) + (t + 1))
                nc.vector.tensor_reduce(row_max[0:QH, j // 2, qt, j % 2:j % 2 + 1], sc[0:QH, at:at + 2, 0:SPAN],
                                        AX.XY, ALU.max).then_inc(max_done, 1)

            def evacuate(it, g, name):
                bank, k = it.pj(g, name)
                dve.wait_ge(hi_done, it.i * (UNITS * 6) + (6 * g + 1 + ["K0", "K1", "Q", "V0", "V1", "V2"].index(name)))
                if name[0] == "V":
                    half, kt = g // 2, 3 * (g % 2) + int(name[1])
                    nc.vector.tensor_tensor(v_sb[:, half, kt, :, DK:2 * DK],
                                            proj[0:KEYS, bank, 0:2 * P].rearrange("p (h d) -> p h d", d=DK),
                                            f32(v_sb[:, half, kt, :, 0:DK]), ALU.subtract).then_inc(proj_taken[bank], 1)
                    return
                if name == "Q":
                    lo, src, hi, bias = q_stage[1], proj[:, bank, 0:SQ], q_stage[0], cols[:, it.layer, 1, g:g + 1]
                else:
                    a, z = K_HALVES[int(name[1])]
                    lo, src, hi, bias = k_stage[1][:, a:z], proj[:, bank, 0:z - a], k_stage[0][:, a:z], cols[:, it.layer, 0, g:g + 1]
                nc.vector.scalar_tensor_tensor(out=lo, in0=src, scalar=bias, in1=f32(hi), op0=ALU.add,
                                               op1=ALU.subtract).then_inc(proj_taken[bank], 1)

            def normalise(it, g):
                w = it.i * UNITS + (g - 2)
                gw = (g - 2) % UNITS
                layer = it.layer if g >= 2 else it.out_layer
                bias = cols[:, layer, 2, gw:gw + 1]
                step = w * NORM_STEPS
                dve.wait_ge(wide_loaded, w * (16 * WIDE_DMAS) + 16 * WIDE_DMAS)
                nc.vector.reciprocal(pv_wide[:, 2, :], pv_wide[:, 2, :]).then_inc(norm_step, 1)
                nc.vector.tensor_tensor(pv_wide[:, 0, :], pv_wide[:, 0, :], pv_wide[:, 1, :], ALU.add).then_inc(norm_step, 1)
                dve.wait_ge(norm_step, step + 2)
                nc.vector.tensor_tensor(pv_wide[:, 0, :], pv_wide[:, 0, :], pv_wide[:, 2, :], ALU.mult).then_inc(norm_step, 1)
                dve.wait_ge(norm_step, step + 3)
                nc.vector.tensor_scalar(a_hi[:, gw, :], pv_wide[:, 0, :], bias, None, ALU.add).then_inc(norm_step, 1)
                dve.wait_ge(norm_step, step + 4)
                nc.vector.scalar_tensor_tensor(out=a_lo[:, gw, :], in0=pv_wide[:, 0, :], scalar=bias, in1=f32(a_hi[:, gw, :]),
                                               op0=ALU.add, op1=ALU.subtract).then_inc(norm_step, 1)

            def add_residual(it, g):
                dve.wait_ge(y_biased, it.i * 2)
                step = it.i * LN_STEPS - LN_STEPS
                for t in range(2):
                    bank, k = it.pj(g, f"O{t}")
                    dve.wait_ge(proj_ready[bank], k + 1)
                    nc.vector.tensor_tensor(y_sb[0:QH, t, :], proj[0:QH, bank, 0:D], y_sb[0:QH, t, :],
                                            ALU.add).then_inc(proj_taken[bank], 1)
                    dve.wait_ge(proj_taken[bank], k + 1)
                    nc.vector.bn_stats(stats[0:QH, t, :], y_sb[0:QH, t, :]).then_inc(ln_step, 1)
                for t in range(2):
                    dve.wait_ge(ln_step, step + (t + 1))
                    dve.sem_inc(stats_seen, 1)
                    nc.vector.bn_aggr(moments[0:QH, t, :], stats[0:QH, t:t + 1, :]).then_inc(ln_step, 1)

            def layer_norm(it):
                step = it.i * LN_STEPS - LN_STEPS
                r = [rstd[0:QH, n, :] for n in range(6)]
                dve.wait_ge(ln_step, step + 4)
                nc.vector.tensor_scalar(r[2], moments[0:QH, :, 1], LN_EPS, None, ALU.add).then_inc(ln_step, 1)
                dve.wait_ge(ln_act, it.i * 2)
                nc.vector.tensor_tensor(r[3], r[1], r[1], ALU.mult).then_inc(ln_step, 1)
                dve.wait_ge(ln_step, step + 6)
                nc.vector.tensor_tensor(r[4], r[3], r[2], ALU.mult).then_inc(ln_step, 1)
                dve.wait_ge(ln_step, step + 7)
                nc.vector.tensor_scalar(r[5], r[4], -0.5, 1.5, ALU.mult, ALU.add).then_inc(ln_step, 1)
                dve.wait_ge(ln_step, step + 8)
                nc.vector.tensor_tensor(r[0], r[1], r[5], ALU.mult).then_inc(ln_step, 1)
                dve.wait_ge(ln_step, step + 9)
                nc.vector.scalar_tensor_tensor(out=r[3], in0=moments[0:QH, :, 0], scalar=-1.0, in1=r[0], op0=ALU.mult,
                                               op1=ALU.mult).then_inc(ln_step, 1)
                dve.wait_ge(ln_step, step + 10)
                for t in range(2):
                    nc.vector.tensor_scalar(y_sb[0:QH, t, :], y_sb[0:QH, t, :], rstd[0:QH, 0, t:t + 1], rstd[0:QH, 3, t:t + 1],
                                            ALU.mult, ALU.add).then_inc(normed, 1)

            dve.wait_ge(consts_loaded, 32)
            for n, (kind, m) in enumerate(FIRST):
                if n % 2 == 0:
                    split_lo(0, n // 2, kind, m)
            dve.wait_ge(selectors_loaded, 16 * 2 * GROUP)
            for it in items(dve):
                for g in range(UNITS):
                    v = it.i * UNITS + (g - 1)
                    normalises = not (it.first and g < 2) and not (it.tail and g > 1)
                    for name in STEPS:
                        if name == "Q" and normalises:
                            normalise(it, g)
                        if not it.does(g, name):
                            continue
                        if name[0] == "S":
                            row_maxima(v, int(name[1]))
                        elif name[0] in "KQV":
                            evacuate(it, g, name)
                        elif name == "O1":
                            add_residual(it, g)
                    if it.attends(g):
                        stack_wait(dve, it, g)
                        pieces = [p for p in pieces_of(it, g)]
                        for c in range(PAIRS):
                            dve.wait_ge(exp_done, v * PAIRS + (c + 1))
                            wait(dve, pv_done, v * PAIRS + (c - 3))
                            nc.vector.tensor_copy(e_hi[0:KEYS, c % 4, :], e_ring[:, c % 3, :]).then_inc(e_hi_done, 1)
                            if LO_ON_DVE[c]:
                                dve.wait_ge(e_hi_done, v * PAIRS + (c + 1))
                                nc.vector.tensor_tensor(e_lo[0:KEYS, c % 4, :], e_ring[:, c % 3, :],
                                                        f32(e_hi[0:KEYS, c % 4, :]), ALU.subtract).then_inc(e_lo_dve, 1)
                            if c == 5 and g == 1 and not it.first:
                                layer_norm(it)
                            if c % 2 == 1 and pieces:
                                n, kind, m = pieces.pop(0)
                                if it.raw(n)[0] == 0:
                                    split_lo(*it.raw(n), kind, m)
                        for n, kind, m in pieces:
                            if it.raw(n)[0] == 0:
                                split_lo(*it.raw(n), kind, m)
                    elif it.tail and g == 1:
                        layer_norm(it)

        @block.gpsimd
        def _(pool):
            def split_lo(slot, k, kind, m):
                pool.wait_ge(raw_hi[slot], k + 1)
                hi, lo = piece_targets(kind, m)
                nc.gpsimd.tensor_tensor(lo, piece_raw(kind, m, slot), f32(hi), ALU.subtract).then_inc(raw_split[slot], 1)

            def add_bias(it):
                pool.wait_ge(rows_loaded, 32 if it.out_layer else 16)
                pool.wait_ge(y_loaded, it.i * 16)
                for t in range(2):
                    nc.gpsimd.tensor_tensor(y_sb[0:QH, t, :], y_sb[0:QH, t, :], rows[0:QH, 0, :], ALU.add).then_inc(y_biased, 1)

            def gamma_beta(it):
                for t in range(2):
                    pool.wait_ge(normed, it.i * 2 - 1 + t)
                    nc.gpsimd.tensor_tensor(y_sb[0:QH, t, :], y_sb[0:QH, t, :], rows[0:QH, 1, :], ALU.mult).then_inc(pool_step, 1)
                    pool.wait_ge(pool_step, it.i * 2 - 1 + t)
                    nc.gpsimd.tensor_tensor(y_sb[0:QH, t, :], y_sb[0:QH, t, :], rows[0:QH, 2, :], ALU.add).then_inc(out_ready, 1)

            nc.gpsimd.memset(f32(k_stack[3 * DK:P, :, :, :]), 0.0).then_inc(zeroed, 1)
            pool.wait_ge(zeroed, 1)
            nc.gpsimd.memset(f32(q_stack[3 * DK:P, :, :, :]), 0.0).then_inc(zeroed, 1)
            pool.wait_ge(zeroed, 2)
            nc.gpsimd.memset(f32(e_hi[0:1, 0:2, :]), 1.0).then_inc(zeroed, 1)
            pool.wait_ge(zeroed, 3)
            nc.gpsimd.memset(f32(v_sb[:, :, :, :, 2 * DK:VCOLS]), 1.0).then_inc(zeroed, 1)
            pool.wait_ge(zeroed, 4)
            nc.gpsimd.memset(eps[:, :], LN_EPS).then_inc(zeroed, 1)
            pool.wait_ge(zeroed, 5)
            for n, (kind, m) in enumerate(FIRST):
                if n % 2 == 1:
                    split_lo(1, n // 2, kind, m)
            for it in items(pool):
                for g in range(UNITS):
                    v = it.i * UNITS + (g - 1)
                    if g == 0 and not it.first:
                        add_bias(it)
                    if it.attends(g):
                        stack_wait(pool, it, g)
                        pieces = pieces_of(it, g)
                        for c in range(PAIRS):
                            if not LO_ON_DVE[c]:
                                pool.wait_ge(e_hi_done, v * PAIRS + (c + 1))
                                wait(pool, pv_done, v * PAIRS + (c - 3))
                                nc.gpsimd.tensor_tensor(e_lo[0:KEYS, c % 4, :], e_ring[:, c % 3, :],
                                                        f32(e_hi[0:KEYS, c % 4, :]), ALU.subtract).then_inc(e_lo_pool, 1)
                            if c % 2 == 1 and pieces:
                                n, kind, m = pieces.pop(0)
                                if it.raw(n)[0] == 1:
                                    split_lo(*it.raw(n), kind, m)
                        for n, kind, m in pieces:
                            if it.raw(n)[0] == 1:
                                split_lo(*it.raw(n), kind, m)
                    if g == 1 and not it.first:
                        gamma_beta(it)


def kernel(**inputs):
    import numpy as np
    import concourse.bacc as bacc
    from concourse.bass_utils import run_bass_kernel_spmd

    a = {name: np.asarray(value) for name, value in inputs.items()}
    x, ctx = a["x"], a["ctx_1024"]
    B, SQ, D = x.shape
    SKV = ctx.shape[1]
    P, KT, DK = 128, D // 128, D // HEADS

    def turned(t):
        return np.ascontiguousarray(t.reshape(t.shape[0], t.shape[1], KT, P).transpose(0, 3, 2, 1))

    def by_dim(w):
        return w.reshape(KT, GROUP, DK, -1).transpose(0, 2, 1, 3).reshape(KT, P, -1)

    def pieces(wq, wk, wv, wo):
        out = []
        for w in (wk, wq):
            out += [w_g.T.reshape(KT, P, P).transpose(1, 0, 2).reshape(P, -1) for w_g in by_dim(w)]
        for half in range(2):
            t = wv[half * D // 2:(half + 1) * D // 2].T.reshape(2, 2, P, D // 2)
            out += [t_k.transpose(1, 0, 2).reshape(P, -1) for t_k in t]
        out += list(by_dim(np.ascontiguousarray(wo.T)))
        return np.stack(out)

    wq, wk, wv = (a["L0_xattn_W_qkv"][n * D:(n + 1) * D] for n in range(3))
    bq, bk, bv = (a["L0_xattn_b_qkv"][n * D:(n + 1) * D] for n in range(3))
    w_pieces = np.stack([pieces(wq, wk, wv, a["L0_xattn_W_o"]),
                         pieces(*(a[f"L1_xattn_W{c}"] for c in "qkvo"))])
    cols = np.stack([np.stack([by_dim(b)[:, :, 0] for b in layer]) for layer in
                     ((bk, bq, bv), tuple(a[f"L1_xattn_b{c}"] for c in "kqv"))])
    rows = np.stack([np.stack([a["L0_xattn_b_o"], a["L0_xattn_ln_gamma"], a["L0_xattn_ln_beta"]]),
                     np.stack([a["L1_xattn_bo"], a["L1_xattn_gamma"], a["L1_xattn_beta"]])])
    arrays = {
        "x": np.ascontiguousarray(x),
        "x_t": turned(x),
        "ctx_t": turned(ctx),
        "w_pieces": np.ascontiguousarray(w_pieces),
        "bias_cols": np.ascontiguousarray(cols.transpose(3, 0, 1, 2)),
        "bias_rows": np.ascontiguousarray(np.broadcast_to(rows[:, None], (LAYERS, P, 3, D))),
        "identity": np.eye(P, dtype=np.float32),
    }
    nc = bacc.Bacc("TRN2", target_bir_lowering=False, num_devices=1)
    args = [nc.dram_tensor(f"in_{name}", t.shape, mybir.dt.from_np(t.dtype), kind="ExternalInput").ap()
            for name, t in arrays.items()]
    args.append(nc.dram_tensor("out", (B, SQ, D), F32, kind="ExternalOutput").ap())
    cross_attention_stack(nc, *args)
    r = run_bass_kernel_spmd(nc, [{f"in_{name}": t for name, t in arrays.items()}], core_ids=[0])
    return r.results[0]["out"]
```

```python
from contextlib import ExitStack

import concourse.bass as bass
from concourse import mybir

F32 = mybir.dt.float32
F32R = mybir.dt.float32r
ALU = mybir.AluOpType
ACT = mybir.ActivationFunctionType
AX = mybir.AxisListType

LAYERS = 2
HEADS = 16
GROUP = 4
UNITS = HEADS // GROUP
LN_EPS = 1e-5

END = "X2 X3 Y0 X4 Y1 X5 Y2 X6 Y3 X7 Y4 X8 Y5 X9 Y6 X10 Y7 X11"
ORDER = [steps.split() for steps in (
    "S0 Y8 S1 Y9 S2 Y10 S3 Y11 S4 V0 S5 M0 V1 S6 K0 S7 V2 K1 X0 X1 Q M1 " + END,
    "S0 Y8 S1 Y9 V0 Y10 S2 Y11 V1 S3 K0 S4 V2 S5 M0 S6 S7 K1 X0 X1 Q M1 " + END,
    "S0 Y8 S1 Y9 V0 Y10 S2 Y11 V1 S3 O0 S4 V2 S5 O1 M0 S6 K0 S7 K1 X0 X1 Q M1 " + END,
    "S0 Y8 S1 Y9 V0 Y10 S2 Y11 V1 S3 K0 T0 S4 V2 S5 K1 M0 S6 S7 Q X0 X1 M1 X2 X3 T1 " + END[6:])]
NORM_AT = (4, 5, 6, 7, 8, 9)
SPLIT_STEPS = (1, 2, 6, 7, 10, 11)


def wait(engine, semaphore, count):
    if not isinstance(count, int) or count > 0:
        engine.wait_ge(semaphore, count)


def cross_attention_stack(nc, x, x_t, ctx_t, w_pieces, bias_cols, bias_rows, identity, out):
    B, SQ, D = x.shape
    P = 128
    KT = D // P
    SKV = ctx_t.shape[3]
    DK = D // HEADS
    KEYS = 125
    NKT = SKV // KEYS
    QH = SQ // 2
    SPAN = 376
    K_HALVES = [(0, SPAN), (SPAN, SKV)]
    ITEMS = LAYERS * B
    PAIRS = GROUP * NKT // 2
    PER_HEAD = NKT // 2
    PAIR = 2 * SQ
    SCALE = float(DK) ** -0.5
    VCOLS = 2 * DK + 1
    PIECE = 512
    assert D == KT * P and SKV == NKT * KEYS and DK * GROUP == P and PAIR <= 512 and 2 * SPAN >= SKV

    LO_ON_DVE = [c in (1, 3, 6, 8, 11) for c in range(PAIRS)]
    N_LO_DVE = sum(LO_ON_DVE)
    N_LO_POOL = PAIRS - N_LO_DVE
    HI_ON_ACT = [c % 3 == 1 for c in range(PAIRS)]
    N_HI_ACT = sum(HI_ON_ACT)
    N_HI_DVE = PAIRS - N_HI_ACT
    LO_ON_POOL = ("V0", "V1", "V2", "K0")
    N_A = 6

    def ordinal(g, name, names):
        return [step for step in ORDER[g] if step in names].index(name) + 1


    FIRST = [("k", 0), ("c", 0), ("c", 1), ("c", 2), ("c", 3), ("q", 0), ("x", 0), ("x", 1), ("v", 0), ("v", 1)]
    REST = {0: [("k", 1), ("q", 1)], 1: [("k", 2), ("q", 2), ("v", 2), ("v", 3)], 2: [("k", 3), ("q", 3)],
            3: [("o", 0), ("o", 1), ("o", 2), ("o", 3)]}
    ITEM_PIECES = [("c", 0), ("c", 1), ("c", 2), ("c", 3), ("x", 0), ("x", 1)]
    REFRESH = {0: [("k", 0), ("q", 0)], 1: [("k", 1), ("q", 1), ("v", 0), ("v", 1)],
               2: [("k", 2), ("q", 2)], 3: [("k", 3), ("q", 3), ("v", 2), ("v", 3)]}
    NP_ITEM = len(ITEM_PIECES)
    NP_REFRESH = sum(len(p) for p in REFRESH.values())
    NP_REST = sum(len(p) for p in REST.values())
    PIECE_INDEX = {**{("k", g): g for g in range(4)}, **{("q", g): 4 + g for g in range(4)},
                   **{("v", n): 8 + n for n in range(4)}, **{("o", k): 12 + k for k in range(4)}}

    x1 = nc.dram_tensor("x1", (B, SQ, D), F32, kind="Internal").ap()
    x1_t = nc.dram_tensor("x1_t", (B, P, KT, SQ), F32, kind="Internal").ap()

    class Item:

        def __init__(self, i, lo, pj0, raw0):
            self.i, self.lo = i, lo
            self.layer = 0 if lo < B else 1
            self.first = lo == 0
            self.tail = lo == ITEMS
            self.refresh = lo == B - 1
            self.refresh_out = lo == B
            self.out_layer = 0 if lo <= B else 1
            self.pj0, self.raw0 = pj0, raw0

        def attends(self, g):
            return not (self.first and g == 0) and not (self.tail and g > 0)

        def finishes(self, g):
            return not (self.first and g < 2) and not (self.tail and g > 1)

        def does(self, g, step):
            if step[0] in "KQV":
                return not self.tail
            if step[0] in "SMX":
                return self.attends(g)
            if step[0] == "Y":
                return self.attends(g) if int(step[1:]) < 8 else self.finishes(g)
            if step[0] == "O":
                return not self.first and g == 2
            return not self.first and self.out_layer == 0 and g == 3

        def groups(self, g):
            return [name for name in ORDER[g] if name[0] in "KQVMOT" and self.does(g, name)]

        def n_groups(self):
            return sum(len(self.groups(g)) for g in range(UNITS))

        def pj(self, g, name):
            n = sum(len(self.groups(h)) for h in range(g)) + self.groups(g).index(name)
            return n % 2, self.pj0 + n // 2

        def n_raw(self):
            return item_raw_at(self) + NP_ITEM * (self.lo < ITEMS - 1)

        def raw(self, n):
            return n % 2, self.raw0 + n // 2

    SEGMENTS = [(0, 1), (1, B - 1), (B - 1, B), (B, B + 1), (B + 1, ITEMS - 1), (ITEMS - 1, ITEMS), (ITEMS, ITEMS + 1)]

    def items(engine):
        pj0, raw0 = 0, len(FIRST) // 2
        for lo, hi in SEGMENTS:
            probe = Item(lo, lo, 0, 0)
            assert probe.n_groups() % 2 == 0 and probe.n_raw() % 2 == 0
            n_pj, n_raw = probe.n_groups() // 2, probe.n_raw() // 2
            if hi - lo == 1:
                yield Item(lo, lo, pj0, raw0)
            else:
                with engine.Fori(lo, hi) as i:
                    yield Item(i, lo, i * n_pj + (pj0 - lo * n_pj), i * n_raw + (raw0 - lo * n_raw))
            pj0 += n_pj * (hi - lo)
            raw0 += n_raw * (hi - lo)

    def item_raw_at(it):
        return NP_REST * it.first + NP_REFRESH * it.refresh + 4 * it.refresh_out

    with ExitStack() as stack:
        def sb(name, shape, dt=F32):
            return stack.enter_context(nc.sbuf_tensor(name, shape, dt))

        def psum(name, shape):
            return stack.enter_context(nc.psum_tensor(name, shape, F32))

        def sem(name):
            return stack.enter_context(nc.semaphore(name))

        w_hi = sb("w_hi", [P, 4, KT, D], F32R)
        w_lo = sb("w_lo", [P, 4, KT, D], F32R)
        c_hi = sb("c_hi", [P, KT, SKV], F32R)
        c_lo = sb("c_lo", [P, KT, SKV], F32R)
        x_hi = sb("x_hi", [P, KT, SQ], F32R)
        x_lo = sb("x_lo", [P, KT, SQ], F32R)
        raw = sb("raw", [P, 2, SKV])
        k_stack = sb("k_stack", [P, 2, GROUP, SKV], F32R)
        q_stack = sb("q_stack", [P, 2, GROUP, SQ], F32R)
        v_sb = sb("v_sb", [KEYS, 2, NKT, 2 * GROUP, VCOLS], F32R)
        e_ring = sb("e_ring", [P, 3, PAIR])
        e_hi = sb("e_hi", [KEYS, 4, PAIR], F32R)
        e_lo = sb("e_lo", [KEYS, 4, PAIR], F32R)
        e_flat = e_ring[:, :, :].rearrange("p a n -> p (a n)")
        v_whole = [e_flat[0:KEYS, n * 2 * P:(n + 1) * 2 * P] for n in range(3)]
        k_whole = e_flat[:, 6 * P:6 * P + SPAN]
        stage = [sb("stage_hi", [P, SKV + SQ], F32R), sb("stage_lo", [P, SKV + SQ], F32R)]
        k_stage = [t[:, 0:SKV] for t in stage]
        q_stage = [t[:, SKV:SKV + SQ] for t in stage]
        row_max = sb("row_max", [P, 2, 2, 2])
        pv_sb = sb("pv_sb", [VCOLS, 2, PAIR])
        pv_wide = sb("pv_wide", [P, 3, SQ])
        a_hi = sb("a_hi", [P, UNITS, SQ], F32R)
        a_lo = sb("a_lo", [P, UNITS, SQ], F32R)
        y_sb = sb("y_sb", [P, 2, D])
        yt_sb = sb("yt_sb", [P, KT, QH])
        cols = sb("cols", [P, LAYERS, 3, UNITS])
        rows = sb("rows", [P, 3, D])
        ident = sb("ident", [P, P])
        eps = sb("eps", [P, 1])
        stats = sb("stats", [P, 2, 6])
        moments = sb("moments", [P, 2, 2])
        rstd = sb("rstd", [P, 6, 2])

        proj = psum("proj", [P, 2, 512])
        sc = psum("sc", [P, 4, 512])
        pv = psum("pv", [P, 2, 512])

        consts_loaded = sem("consts_loaded")
        rows_loaded = sem("rows_loaded")
        piece_loaded = {piece: sem("loaded_%s%d" % piece) for piece in list(PIECE_INDEX) + ITEM_PIECES}
        raw_hi = [sem(f"raw_hi{n}") for n in range(2)]
        raw_split = [sem(f"raw_split{n}") for n in range(2)]
        zeroed = sem("zeroed")
        selectors_loaded = sem("selectors_loaded")
        proj_ready = [sem(f"proj_ready{n}") for n in range(2)]
        hi_done = sem("hi_done")
        lo_done = sem("lo_done")
        proj_taken = [sem(f"proj_taken{n}") for n in range(2)]
        stack_loaded = [sem(f"stack_loaded{n}") for n in range(2)]
        scores_ready = sem("scores_ready")
        max_done = sem("max_done")
        shifted_ready = sem("shifted_ready")
        exp_done = sem("exp_done")
        e_hi_act = sem("e_hi_act")
        e_hi_dve = sem("e_hi_dve")
        e_lo_dve = sem("e_lo_dve")
        e_lo_pool = sem("e_lo_pool")
        pv_done = sem("pv_done")
        pv_taken = sem("pv_taken")
        wide_loaded = sem("wide_loaded")
        norm_step = sem("norm_step")
        y_loaded = sem("y_loaded")
        y_biased = sem("y_biased")
        ln_step = sem("ln_step")
        ln_act = sem("ln_act")
        stats_seen = sem("stats_seen")
        normed = sem("normed")
        pool_step = sem("pool_step")
        out_ready = sem("out_ready")
        out_stored = sem("out_stored")
        yt_stored = sem("yt_stored")

        block = stack.enter_context(nc.Block())

        STACK_DMAS = 6
        WIDE_DMAS = 6
        NORM_STEPS = 6
        LN_STEPS = 10
        f32 = lambda ap: ap.bitcast(F32)
        q_ones = stage[1][0:1, 0:SKV]

        def piece_columns(kind, n):
            return {"c": SKV, "x": 2 * SQ}.get(kind, PIECE)

        def piece_source(kind, n, item, layer):
            if kind == "c":
                return ctx_t[item - B if layer else item, :, n, :]
            if kind == "x":
                return (x1_t[item - B] if layer else x_t[item])[:, 2 * n:2 * n + 2, :]
            return w_pieces[layer, PIECE_INDEX[kind, n]]

        def piece_targets(kind, n):
            if kind == "c":
                return [t[:, n, :] for t in (c_hi, c_lo)]
            if kind == "x":
                return [t[:, 2 * n:2 * n + 2, :] for t in (x_hi, x_lo)]
            if kind in "kq":
                return [t[:, "kq".index(kind), :, n * P:(n + 1) * P] for t in (w_hi, w_lo)]
            if kind == "v":
                half, k = divmod(n, 2)
                return [t[:, 2, 2 * k:2 * k + 2, half * 2 * P:(half + 1) * 2 * P] for t in (w_hi, w_lo)]
            return [t[:, 3, n, :] for t in (w_hi, w_lo)]

        def flat(t):
            return t[:, :, :].rearrange("p a n -> p (a n)")

        FIRST_AT = [y_sb[:, 0, :], raw[:, 1, :], raw[:, 0, :], e_flat[:, 0:SKV], flat(rows)[:, 0:SKV], y_sb[:, 1, :],
                    flat(yt_sb), e_flat[:, SKV:SKV + 2 * SQ], flat(rows)[:, SKV:SKV + PIECE], flat(pv_wide)[:, 0:PIECE]]

        def piece_raw(kind, n, place):
            if kind == "c" or kind == "o":
                return place
            return place.rearrange("p (a n) -> p a n", a=4 if kind in "kq" else 2)

        def raw_slot(it, n, kind):
            return raw[:, it.raw(n)[0], 0:piece_columns(kind, n)]

        def pieces_of(it, g):
            found = []
            if it.first or it.refresh:
                table = REST if it.first else REFRESH
                at = sum(len(table[h]) for h in range(g))
                found += [(at + m, *p) for m, p in enumerate(table[g])]
            if it.refresh_out and g == 2:
                found += [(m, "o", m) for m in range(4)]
            if g == 3 and it.lo < ITEMS - 1:
                found += [(item_raw_at(it) + m, *p) for m, p in enumerate(ITEM_PIECES)]
            return found

        def last_reader(it, g, kind):
            return it.pj(g, {"o": "O1", "v": "V2", "k": "K1", "c": "K1"}.get(kind, "Q"))

        def hi_ready(engine, v, c):
            v, c = (v, c) if c >= 0 else (v - 1, c + PAIRS)
            n = sum(HI_ON_ACT[:c + 1])
            if HI_ON_ACT[c]:
                wait(engine, e_hi_act, v * N_HI_ACT + n)
            else:
                wait(engine, e_hi_dve, v * N_HI_DVE + c + 1 - n)

        def lo_ready(engine, v, c):
            v, c = (v, c) if c >= 0 else (v - 1, c + PAIRS)
            n = sum(LO_ON_DVE[:c + 1])
            if LO_ON_DVE[c]:
                wait(engine, e_lo_dve, v * N_LO_DVE + n)
            else:
                wait(engine, e_lo_pool, v * N_LO_POOL + c + 1 - n)

        @block.sync
        def _(sp):
            sp.dma_start(cols[:, :, :, :], bias_cols).then_inc(consts_loaded, 16)
            sp.dma_start(ident[:, :], identity).then_inc(consts_loaded, 16)

            def load(kind, m, place, item, layer):
                sp.dma_start(piece_raw(kind, m, place), piece_source(kind, m, item, layer)).then_inc(piece_loaded[kind, m], 16)

            for n, (kind, m) in enumerate(FIRST):
                load(kind, m, FIRST_AT[n], 0, 0)
                if n == 4:
                    sp.wait_ge(zeroed, 3)
                    for b in range(2):
                        for j in range(GROUP):
                            r = 3 * DK + j % 2
                            sp.dma_start(f32(k_stack[r:r + 1, b, j, :]), f32(q_ones)).then_inc(selectors_loaded, 16)

            for turn in range(2):
                sp.wait_ge(raw_split[turn], len(FIRST) // 2)
            sp.dma_start(rows[:, :, :], bias_rows[0]).then_inc(rows_loaded, 16)

            for it in items(sp):
                value = (lambda v: v) if isinstance(it.i, int) else sp.snap
                if not it.tail:
                    lo_count = {g: value(it.i * (len(LO_ON_POOL) * UNITS) + (len(LO_ON_POOL) * g + ordinal(g, "K0", LO_ON_POOL)))
                                for g in range(UNITS)}
                    taken = {(g, name): value(it.pj(g, name)[1] + 1) for g in range(UNITS) for name in ("K1", "Q")}
                    free = [value(it.raw(n)[1]) for n in range(it.n_raw())]
                pv_count = [value(it.i * (2 * UNITS) + 2 * (g - 1)) for g in range(UNITS)]
                twice = value(it.i * 2)
                turned = {t: value(it.pj(3, f"T{t}")[1] + 1) for t in range(2) if it.does(3, f"T{t}")}
                stored = value(it.i * 32)
                for g in range(UNITS):
                    b = g % 2
                    if it.finishes(g):
                        sp.wait_ge(pv_taken, pv_count[g])
                        for part in range(2):
                            src = pv_sb[part * DK:(part + 1) * DK, :, :].rearrange("d a (b q) -> d (a b) q", b=2)
                            sp.dma_start(pv_wide[:, part, :], src).then_inc(wide_loaded, 16)
                        for j in range(GROUP):
                            one = pv_sb[2 * DK:2 * DK + 1, :, :]
                            src = bass.AP(one.tensor, one.offset + j * SQ, [[2 * PAIR, 1], [0, DK], [1, SQ]])
                            sp.dma_start(pv_wide[j:P:GROUP, 2, :], src).then_inc(wide_loaded, 16)
                    pieces = pieces_of(it, g)

                    def load_pieces(some):
                        for n, kind, m in some:
                            sp.wait_ge(raw_split[it.raw(n)[0]], free[n])
                            load(kind, m, raw_slot(it, n, kind), it.i + 1, int(it.lo >= B - 1))

                    load_pieces(pieces[:2])
                    if not it.first and g == (2 if it.tail else 3):
                        sp.wait_ge(out_ready, twice)
                        dst = out[it.i - 1 - B] if it.out_layer else x1[it.i - 1]
                        for t in range(2):
                            sp.dma_start(dst[t * QH:(t + 1) * QH, :], y_sb[0:QH, t, :]).then_inc(out_stored, 16)
                        if it.refresh_out:
                            sp.dma_start(rows[:, :, :], bias_rows[1]).then_inc(rows_loaded, 16)

                    def store_turned(t):
                        if t in turned:
                            sp.wait_ge(proj_taken[it.pj(g, f"T{t}")[0]], turned[t])
                            sp.dma_start(x1_t[it.i - 1, :, :, t * QH:(t + 1) * QH], yt_sb[:, :, :]).then_inc(yt_stored, 16)

                    if g == 3:
                        store_turned(0)

                    if not it.tail:
                        sp.wait_ge(proj_taken[it.pj(g, "K1")[0]], taken[g, "K1"])
                        for r in (0, DK):
                            sp.dma_start(f32(k_stack[r:r + DK, b, :, :]), f32(k_stage[0])).then_inc(stack_loaded[b], 16)
                        sp.wait_ge(lo_done, lo_count[g])
                        sp.dma_start(f32(k_stack[2 * DK:3 * DK, b, :, :]), f32(k_stage[1])).then_inc(stack_loaded[b], 16)
                        sp.wait_ge(proj_taken[it.pj(g, "Q")[0]], taken[g, "Q"])
                        for r, part in ((0, 0), (DK, 1), (2 * DK, 0)):
                            sp.dma_start(f32(q_stack[r:r + DK, b, :, :]), f32(q_stage[part])).then_inc(stack_loaded[b], 16)
                    load_pieces(pieces[2:])
                    if g == 3:
                        store_turned(1)
                    if g == 3 and not it.tail:
                        wait(sp, out_stored, stored)
                        if it.out_layer == 0:
                            wait(sp, yt_stored, stored)
                        src = x1[it.i - B] if it.layer else x[it.i]
                        sp.dma_start(y_sb[0:QH, :, :], src.rearrange("(t q) d -> q t d", q=QH)).then_inc(y_loaded, 16)
            sp.wait_ge(out_stored, 32 * ITEMS)
            sp.wait_ge(yt_stored, 32 * B)

        @block.tensor
        def _(pe):
            def free_bank(it, g, name):
                bank, k = it.pj(g, name)
                wait(pe, proj_taken[bank], k)
                return bank

            def three_passes(target, w, w2, a, a2, k):
                nc.tensor.matmul(target, w, a, start=(k == 0), stop=False)
                nc.tensor.matmul(target, w2, a, start=False, stop=False)
                return nc.tensor.matmul(target, w, a2, start=False, stop=(k == KT - 1))

            def first_split(it, n):
                if it.first:
                    pe.wait_ge(raw_split[n % 2], n // 2 + 1)
                    pe.wait_ge(raw_split[1 - n % 2], (n + 1) // 2)

            def project_keys(it, g, half):
                first_split(it, [4, 10, 12, 16][g])
                lo, hi = K_HALVES[half]
                bank = free_bank(it, g, f"K{half}")
                for k in range(KT):
                    cs = slice(g * P, (g + 1) * P)
                    mm = three_passes(proj[:, bank, 0:hi - lo], w_hi[:, 0, k, cs], w_lo[:, 0, k, cs],
                                      c_hi[:, k, lo:hi], c_lo[:, k, lo:hi], k)
                mm.then_inc(proj_ready[bank], 1)

            def project_queries(it, g):
                first_split(it, [7, 11, 13, 17][g])
                if not it.first and g == 0:
                    for slot in range(2):
                        pe.wait_ge(raw_split[slot], it.raw0)
                bank = free_bank(it, g, "Q")
                for k in range(KT):
                    cs = slice(g * P, (g + 1) * P)
                    mm = three_passes(proj[:, bank, 0:SQ], w_hi[:, 1, k, cs], w_lo[:, 1, k, cs],
                                      x_hi[:, k, :], x_lo[:, k, :], k)
                mm.then_inc(proj_ready[bank], 1)

            def project_values(it, g, n):
                first_split(it, [9, 9, 15, 15][g])
                if not it.first and g == 0 and n == 0:
                    for slot in range(2):
                        pe.wait_ge(raw_split[slot], it.raw0 - 1)
                half, kt = g // 2, 3 * (g % 2) + n
                bank = free_bank(it, g, f"V{n}")
                ks = slice(kt * KEYS, (kt + 1) * KEYS)
                ds = slice(half * 2 * P, (half + 1) * 2 * P)
                for k in range(KT):
                    mm = three_passes(proj[0:KEYS, bank, 0:2 * P], c_hi[:, k, ks], c_lo[:, k, ks],
                                      w_hi[:, 2, k, ds], w_lo[:, 2, k, ds], k)
                mm.then_inc(proj_ready[bank], 1)

            def scores(v, t, b):
                j, qt = divmod(t, 2)
                if t < 2:
                    wait(pe, exp_done, v * PAIRS - (2 if t == 0 else 0))
                else:
                    pe.wait_ge(max_done, v * (2 * GROUP) + (t - 1))
                q = q_stack[0:3 * DK, b, j, qt * QH:(qt + 1) * QH]
                at = 2 * (t % 2)
                nc.tensor.matmul(sc[0:QH, at, 0:SPAN], q, k_stack[0:3 * DK, b, j, 0:SPAN], start=True, stop=True)
                nc.tensor.matmul(sc[0:QH, at + 1, 0:SPAN], q, k_stack[0:3 * DK, b, j, SKV - SPAN:SKV],
                                 start=True, stop=True).then_inc(scores_ready, 1)

            def turn_maxima(it, g, v, pair):
                bank = free_bank(it, g, f"M{pair}")
                pe.wait_ge(max_done, v * (2 * GROUP) + 4 * (pair + 1))
                for qt in range(2):
                    mm = nc.tensor.transpose(proj[0:2, bank, qt * QH:(qt + 1) * QH], row_max[0:QH, pair, qt, :],
                                             ident[0:QH, 0:QH])
                mm.then_inc(proj_ready[bank], 1)

            def shifted_scores(it, g, v, c, b):
                j, m = divmod(c, PER_HEAD)
                if c in (0, 2 * PER_HEAD):
                    bank, k = it.pj(g, f"M{c // (2 * PER_HEAD)}")
                    pe.wait_ge(proj_taken[bank], k + 1)
                if c in (0, 2):
                    pe.wait_ge(max_done, v * (2 * GROUP) + (2 * GROUP - 1 + c // 2))
                if c >= 4:
                    pe.wait_ge(exp_done, v * PAIRS + (c - 3))
                for n in range(2):
                    ks = slice((2 * m + n) * KEYS, (2 * m + n + 1) * KEYS)
                    mm = nc.tensor.matmul(sc[0:KEYS, c % 4, n * SQ:(n + 1) * SQ], k_stack[:, b, j, ks], q_stack[:, b, j, :],
                                          start=True, stop=True)
                mm.then_inc(shifted_ready, 1)

            def times_values(v, c, gv):
                j, m = divmod(c, PER_HEAD)
                if c in (0, 2 * PER_HEAD):
                    wait(pe, pv_taken, v * 2 - 1 + c // (2 * PER_HEAD))
                hi_ready(pe, v, c)
                lo_ready(pe, v, c)
                for n in range(2):
                    kt = 2 * m + n
                    target = pv[0:VCOLS, j // 2, (j % 2) * SQ:(j % 2 + 1) * SQ]
                    values = v_sb[:, gv // 2, kt, GROUP * (gv % 2) + j, :]
                    nc.tensor.matmul(target, values, e_hi[0:KEYS, c % 4, n * SQ:(n + 1) * SQ], start=(kt == 0), stop=False)
                    mm = nc.tensor.matmul(target, values, e_lo[0:KEYS, c % 4, n * SQ:(n + 1) * SQ],
                                          start=False, stop=(kt == NKT - 1))
                mm.then_inc(pv_done, 1)

            def project_out(it, g, t):
                bank = free_bank(it, g, f"O{t}")
                pe.wait_ge(norm_step, it.i * (UNITS * NORM_STEPS))
                qs = slice(t * QH, (t + 1) * QH)
                for k in range(KT):
                    mm = three_passes(proj[0:QH, bank, 0:D], a_hi[:, k, qs], a_lo[:, k, qs],
                                      w_hi[:, 3, k, :], w_lo[:, 3, k, :], k)
                mm.then_inc(proj_ready[bank], 1)

            def turn_output(it, g, t):
                bank = free_bank(it, g, f"T{t}")
                pe.wait_ge(out_ready, it.i * 2 - 1 + t)
                for k in range(KT):
                    mm = nc.tensor.transpose(proj[:, bank, k * QH:(k + 1) * QH], y_sb[0:QH, t, k * P:(k + 1) * P],
                                             ident[0:QH, 0:QH])
                mm.then_inc(proj_ready[bank], 1)

            pe.wait_ge(consts_loaded, 32)
            pe.wait_ge(zeroed, 5)
            pe.wait_ge(selectors_loaded, 16 * 2 * GROUP)
            for it in items(pe):
                for g in range(UNITS):
                    v = it.i * UNITS + (g - 1)
                    b = (g + 1) % 2
                    for step in ORDER[g]:
                        if not it.does(g, step):
                            continue
                        n = int(step[1:] or 0)
                        if step == "S0":
                            pe.wait_ge(stack_loaded[b], (it.i * 2 + ((g - 1) // 2 + 1)) * (16 * STACK_DMAS))
                        if step == "Y0" and not it.tail:
                            pe.wait_ge(lo_done, it.i * (len(LO_ON_POOL) * UNITS) + len(LO_ON_POOL) * (g + 1))
                        if step[0] == "S":
                            scores(v, n, b)
                        elif step[0] == "M":
                            turn_maxima(it, g, v, n)
                        elif step[0] == "X":
                            shifted_scores(it, g, v, n, b)
                        elif step[0] == "Y":
                            if n < 8:
                                times_values(v, n, (g - 1) % UNITS)
                            else:
                                times_values(it.i * UNITS + (g - 2), n, (g - 2) % UNITS)
                        elif step[0] == "K":
                            project_keys(it, g, n)
                        elif step[0] == "Q":
                            project_queries(it, g)
                        elif step[0] == "V":
                            project_values(it, g, n)
                        elif step[0] == "O":
                            project_out(it, g, n)
                        else:
                            turn_output(it, g, n)

        @block.scalar
        def _(act):
            act.preload_act_table_set("natural_log_exp_and_others")

            def split_hi(turn, count, kind, m, place):
                act.wait_ge(piece_loaded[kind, m], count)
                nc.scalar.activation(piece_targets(kind, m)[0], piece_raw(kind, m, place), ACT.Copy).then_inc(raw_hi[turn], 1)

            def split_piece(it, g, piece):
                n, kind, m = piece
                if not it.first or kind in "cx":
                    bank, k = last_reader(it, g, kind)
                    act.wait_ge(proj_ready[bank], k + 1)
                count = it.i * 16 + 32 if kind in "cx" else 16 * (1 + (it.lo > 0))
                split_hi(it.raw(n)[0], count, kind, m, raw_slot(it, n, kind))

            def evacuate(it, g, name):
                bank, k = it.pj(g, name)
                act.wait_ge(proj_ready[bank], k + 1)
                bias, whole = 0.0, None
                if name[0] == "V":
                    half, kt = g // 2, 3 * (g % 2) + int(name[1])
                    hi = v_sb[:, half, kt, :, 0:DK]
                    whole = v_whole[int(name[1])].rearrange("p (h d) -> p h d", d=DK)
                    src = proj[0:KEYS, bank, 0:2 * P].rearrange("p (h d) -> p h d", d=DK)
                elif name == "Q":
                    hi, src, bias = q_stage[0], proj[:, bank, 0:SQ], cols[:, it.layer, 1, g:g + 1]
                else:
                    a, z = K_HALVES[int(name[1])]
                    hi, src, bias = k_stage[0][:, a:z], proj[:, bank, 0:z - a], cols[:, it.layer, 0, g:g + 1]
                    whole = k_whole
                if name == "K0" and not (it.first and g == 0):
                    act.wait_ge(stack_loaded[(g + 1) % 2], (it.i * 2 + ((g - 1) // 2 + 1)) * (16 * STACK_DMAS))
                nc.scalar.activation(hi, src, ACT.Identity, bias=bias).then_inc(hi_done, 1)
                if name not in LO_ON_POOL:
                    return
                if ordinal(g, name, LO_ON_POOL) == 1 and it.finishes(g):
                    for c in (PAIRS - 3, PAIRS - 2, PAIRS - 1):
                        lo_ready(act, it.i * UNITS + (g - 2), c)
                if name == "V0" and it.first and g == 1:
                    act.wait_ge(lo_done, len(LO_ON_POOL))
                nc.scalar.activation(whole, src, ACT.Identity, bias=bias).then_inc(proj_taken[bank], 1)

            def maxima_rows(it, g, pair, b):
                bank, k = it.pj(g, f"M{pair}")
                act.wait_ge(proj_ready[bank], k + 1)
                turned = proj[0:2, bank, 0:SQ].unsqueeze(1).broadcast_to([2, 2, SQ])
                nc.scalar.activation(q_stack[3 * DK:3 * DK + 2, b, 2 * pair:2 * pair + 2, :], turned, ACT.Copy,
                                     scale=-1.0).then_inc(proj_taken[bank], 1)

            def exponentials(it, g, v, c):
                act.wait_ge(shifted_ready, v * PAIRS + (c + 1))
                src = sc[0:KEYS, c % 4, 0:PAIR]
                if HI_ON_ACT[c]:
                    wait(act, pv_done, v * PAIRS + (c - 3))
                    nc.scalar.activation(e_hi[:, c % 4, :], src, ACT.Exp, scale=SCALE).then_inc(e_hi_act, 1)
                if c == 0 and not it.tail:
                    act.wait_ge(lo_done, it.i * (len(LO_ON_POOL) * UNITS) + len(LO_ON_POOL) * (g + 1))
                hi_ready(act, v, c - 3)
                lo_ready(act, v, c - 3)
                nc.scalar.activation(e_ring[0:KEYS, c % 3, :], src, ACT.Exp, scale=SCALE).then_inc(exp_done, 1)

            def take_products(v, n):
                act.wait_ge(pv_done, v * PAIRS + 2 * PER_HEAD * (n + 1))
                wait(act, wide_loaded, v * (16 * WIDE_DMAS))
                nc.scalar.activation(pv_sb[:, n, :], pv[0:VCOLS, n, 0:PAIR], ACT.Copy).then_inc(pv_taken, 1)

            def deviation(it):
                act.wait_ge(ln_step, it.i * LN_STEPS - (LN_STEPS - 4))
                nc.scalar.activation(rstd[0:QH, 0, :], moments[0:QH, :, 1], ACT.Ln, bias=eps[0:QH, :]).then_inc(ln_act, 1)
                act.wait_ge(ln_act, it.i * 2 - 1)
                nc.scalar.activation(rstd[0:QH, 1, :], rstd[0:QH, 0, :], ACT.Exp, scale=-0.5).then_inc(ln_act, 1)

            for n, (kind, m) in enumerate(FIRST):
                split_hi(n % 2, 16, kind, m, FIRST_AT[n])
            act.wait_ge(consts_loaded, 32)
            act.wait_ge(zeroed, 5)
            act.wait_ge(selectors_loaded, 16 * 2 * GROUP)
            for it in items(act):
                for g in range(UNITS):
                    v = it.i * UNITS + (g - 1)
                    b = (g + 1) % 2
                    pieces = pieces_of(it, g)
                    for step in ORDER[g]:
                        if not it.does(g, step):
                            continue
                        n = int(step[1:] or 0)
                        if step[0] in "KQV":
                            evacuate(it, g, step)
                        elif step == "Y11":
                            take_products(it.i * UNITS + (g - 2), 1)
                        elif step[0] == "M":
                            maxima_rows(it, g, n, b)
                        elif step[0] == "T":
                            bank, k = it.pj(g, step)
                            act.wait_ge(proj_ready[bank], k + 1)
                            if step == "T1":
                                act.wait_ge(yt_stored, it.i * 32 - 16)
                            nc.scalar.activation(yt_sb[:, :, :], proj[:, bank, 0:KT * QH].rearrange("p (k q) -> p k q", q=QH),
                                                 ACT.Copy).then_inc(proj_taken[bank], 1)
                        elif step[0] == "X":
                            exponentials(it, g, v, n)
                            if n == 3 and g == 2 and not it.first:
                                deviation(it)
                            if n == 9:
                                take_products(v, 0)
                            if n in SPLIT_STEPS and pieces:
                                split_piece(it, g, pieces.pop(0))
                    for piece in pieces:
                        split_piece(it, g, piece)
                    if it.tail and g == 2:
                        deviation(it)

        @block.vector
        def _(dve):
            def split_lo(turn, k, kind, m, place):
                dve.wait_ge(raw_hi[turn], k + 1)
                hi, lo = piece_targets(kind, m)
                nc.vector.tensor_tensor(lo, piece_raw(kind, m, place), f32(hi), ALU.subtract).then_inc(raw_split[turn], 1)

            def split_piece(it, piece):
                n, kind, m = piece
                if it.raw(n)[0] == 0:
                    split_lo(*it.raw(n), kind, m, raw_slot(it, n, kind))

            def row_maxima(v, t):
                j, qt = divmod(t, 2)
                at = 2 * (t % 2)
                dve.wait_ge(scores_ready, v * (2 * GROUP) + (t + 1))
                nc.vector.tensor_reduce(row_max[0:QH, j // 2, qt, j % 2:j % 2 + 1], sc[0:QH, at:at + 2, 0:SPAN],
                                        AX.XY, ALU.max).then_inc(max_done, 1)

            def projection_lo(it, g, name):
                bank, k = it.pj(g, name)
                if name == "Q":
                    (hi, lo), src, bias = q_stage, proj[:, bank, 0:SQ], cols[:, it.layer, 1, g:g + 1]
                else:
                    a, z = K_HALVES[int(name[1])]
                    hi, lo = (t[:, a:z] for t in k_stage)
                    src, bias = proj[:, bank, 0:z - a], cols[:, it.layer, 0, g:g + 1]
                dve.wait_ge(hi_done, it.i * (N_A * UNITS) + (N_A * g + ordinal(g, name, ("V0", "V1", "V2", "K0", "K1", "Q"))))
                nc.vector.scalar_tensor_tensor(out=lo, in0=src, scalar=bias, in1=f32(hi), op0=ALU.add,
                                               op1=ALU.subtract).then_inc(proj_taken[bank], 1)

            def halves(v, c):
                ring, at = e_ring[0:KEYS, c % 3, :], c % 4
                if not (HI_ON_ACT[c] and not LO_ON_DVE[c]):
                    dve.wait_ge(exp_done, v * PAIRS + (c + 1))
                    wait(dve, pv_done, v * PAIRS + (c - 3))
                if not HI_ON_ACT[c]:
                    nc.vector.tensor_copy(e_hi[:, at, :], ring).then_inc(e_hi_dve, 1)
                if LO_ON_DVE[c]:
                    hi_ready(dve, v, c)
                    nc.vector.tensor_tensor(e_lo[:, at, :], ring, f32(e_hi[:, at, :]), ALU.subtract).then_inc(e_lo_dve, 1)

            def normalise(it, g, part):
                w = it.i * UNITS + (g - 2)
                gw = (g - 2) % UNITS
                bias = cols[:, it.layer if g >= 2 else it.out_layer, 2, gw:gw + 1]
                if part > 2:
                    dve.wait_ge(norm_step, w * NORM_STEPS + part)
                if part < 2:
                    if part == 0:
                        dve.wait_ge(wide_loaded, w * (16 * WIDE_DMAS) + 16 * WIDE_DMAS)
                    half = pv_wide[:, 2, part * QH:(part + 1) * QH]
                    op = nc.vector.reciprocal(half, half)
                elif part == 2:
                    op = nc.vector.tensor_tensor(pv_wide[:, 0, :], pv_wide[:, 0, :], pv_wide[:, 1, :], ALU.add)
                elif part == 3:
                    op = nc.vector.tensor_tensor(pv_wide[:, 0, :], pv_wide[:, 0, :], pv_wide[:, 2, :], ALU.mult)
                elif part == 4:
                    op = nc.vector.tensor_scalar(a_hi[:, gw, :], pv_wide[:, 0, :], bias, None, ALU.add)
                else:
                    op = nc.vector.scalar_tensor_tensor(out=a_lo[:, gw, :], in0=pv_wide[:, 0, :], scalar=bias,
                                                        in1=f32(a_hi[:, gw, :]), op0=ALU.add, op1=ALU.subtract)
                op.then_inc(norm_step, 1)

            def add_residual(it, g):
                dve.wait_ge(y_biased, it.i * 2)
                step = it.i * LN_STEPS - LN_STEPS
                for t in range(2):
                    bank, k = it.pj(g, f"O{t}")
                    dve.wait_ge(proj_ready[bank], k + 1)
                    nc.vector.tensor_tensor(y_sb[0:QH, t, :], proj[0:QH, bank, 0:D], y_sb[0:QH, t, :],
                                            ALU.add).then_inc(proj_taken[bank], 1)
                    dve.wait_ge(proj_taken[bank], k + 1)
                    nc.vector.bn_stats(stats[0:QH, t, :], y_sb[0:QH, t, :]).then_inc(ln_step, 1)
                for t in range(2):
                    dve.wait_ge(ln_step, step + (t + 1))
                    dve.sem_inc(stats_seen, 1)
                    nc.vector.bn_aggr(moments[0:QH, t, :], stats[0:QH, t:t + 1, :]).then_inc(ln_step, 1)

            def layer_norm(it):
                step = it.i * LN_STEPS - LN_STEPS
                r = [rstd[0:QH, n, :] for n in range(6)]
                dve.wait_ge(ln_step, step + 4)
                nc.vector.tensor_scalar(r[2], moments[0:QH, :, 1], LN_EPS, None, ALU.add).then_inc(ln_step, 1)
                dve.wait_ge(ln_act, it.i * 2)
                nc.vector.tensor_tensor(r[3], r[1], r[1], ALU.mult).then_inc(ln_step, 1)
                dve.wait_ge(ln_step, step + 6)
                nc.vector.tensor_tensor(r[4], r[3], r[2], ALU.mult).then_inc(ln_step, 1)
                dve.wait_ge(ln_step, step + 7)
                nc.vector.tensor_scalar(r[5], r[4], -0.5, 1.5, ALU.mult, ALU.add).then_inc(ln_step, 1)
                dve.wait_ge(ln_step, step + 8)
                nc.vector.tensor_tensor(r[0], r[1], r[5], ALU.mult).then_inc(ln_step, 1)
                dve.wait_ge(ln_step, step + 9)
                nc.vector.scalar_tensor_tensor(out=r[3], in0=moments[0:QH, :, 0], scalar=-1.0, in1=r[0], op0=ALU.mult,
                                               op1=ALU.mult).then_inc(ln_step, 1)
                dve.wait_ge(ln_step, step + 10)
                for t in range(2):
                    nc.vector.tensor_scalar(y_sb[0:QH, t, :], y_sb[0:QH, t, :], rstd[0:QH, 0, t:t + 1], rstd[0:QH, 3, t:t + 1],
                                            ALU.mult, ALU.add).then_inc(normed, 1)

            dve.wait_ge(consts_loaded, 32)
            for n, (kind, m) in enumerate(FIRST):
                if n % 2 == 0:
                    split_lo(0, n // 2, kind, m, FIRST_AT[n])
            for it in items(dve):
                for g in range(UNITS):
                    v = it.i * UNITS + (g - 1)
                    pieces = pieces_of(it, g)
                    for step in ORDER[g]:
                        if not it.does(g, step):
                            continue
                        n = int(step[1:] or 0)
                        if step[0] == "S":
                            row_maxima(v, n)
                        elif step in ("K1", "Q"):
                            projection_lo(it, g, step)
                        elif step == "O1":
                            add_residual(it, g)
                        elif step[0] == "X":
                            halves(v, n)
                            if n in NORM_AT and it.finishes(g):
                                normalise(it, g, NORM_AT.index(n))
                            if n == 7 and g == 2 and not it.first:
                                layer_norm(it)
                            if n in SPLIT_STEPS and pieces:
                                split_piece(it, pieces.pop(0))
                    for piece in pieces:
                        split_piece(it, piece)
                    if it.tail and g == 1:
                        for part in range(NORM_STEPS):
                            normalise(it, g, part)
                    if it.tail and g == 2:
                        layer_norm(it)

        @block.gpsimd
        def _(pool):
            def split_lo(turn, k, kind, m, place):
                pool.wait_ge(raw_hi[turn], k + 1)
                hi, lo = piece_targets(kind, m)
                nc.gpsimd.tensor_tensor(lo, piece_raw(kind, m, place), f32(hi), ALU.subtract).then_inc(raw_split[turn], 1)

            def split_piece(it, piece):
                n, kind, m = piece
                if it.raw(n)[0] == 1:
                    split_lo(*it.raw(n), kind, m, raw_slot(it, n, kind))

            def projection_lo(it, g, name):
                bank, k = it.pj(g, name)
                pool.wait_ge(proj_taken[bank], k + 1)
                if name[0] == "V":
                    half, kt = g // 2, 3 * (g % 2) + int(name[1])
                    hi, lo = v_sb[:, half, kt, :, 0:DK], v_sb[:, half, kt, :, DK:2 * DK]
                    whole = v_whole[int(name[1])].rearrange("p (h d) -> p h d", d=DK)
                else:
                    hi, lo, whole = k_stage[0][:, 0:SPAN], k_stage[1][:, 0:SPAN], k_whole
                nc.gpsimd.tensor_tensor(lo, whole, f32(hi), ALU.subtract).then_inc(lo_done, 1)

            def exponentials_lo(v, c):
                hi_ready(pool, v, c)
                pool.wait_ge(exp_done, v * PAIRS + (c + 1))
                wait(pool, pv_done, v * PAIRS + (c - 3))
                nc.gpsimd.tensor_tensor(e_lo[:, c % 4, :], e_ring[0:KEYS, c % 3, :], f32(e_hi[:, c % 4, :]),
                                        ALU.subtract).then_inc(e_lo_pool, 1)

            def add_bias(it):
                pool.wait_ge(rows_loaded, 32 if it.out_layer else 16)
                pool.wait_ge(y_loaded, it.i * 16)
                for t in range(2):
                    nc.gpsimd.tensor_tensor(y_sb[0:QH, t, :], y_sb[0:QH, t, :], rows[0:QH, 0, :], ALU.add).then_inc(y_biased, 1)

            def gamma_beta(it):
                for t in range(2):
                    pool.wait_ge(normed, it.i * 2 - 1 + t)
                    nc.gpsimd.tensor_tensor(y_sb[0:QH, t, :], y_sb[0:QH, t, :], rows[0:QH, 1, :], ALU.mult).then_inc(pool_step, 1)
                    pool.wait_ge(pool_step, it.i * 2 - 1 + t)
                    nc.gpsimd.tensor_tensor(y_sb[0:QH, t, :], y_sb[0:QH, t, :], rows[0:QH, 2, :], ALU.add).then_inc(out_ready, 1)

            nc.gpsimd.memset(f32(k_stack[3 * DK:P, :, :, :]), 0.0).then_inc(zeroed, 1)
            pool.wait_ge(zeroed, 1)
            nc.gpsimd.memset(f32(q_stack[3 * DK:P, :, :, :]), 0.0).then_inc(zeroed, 1)
            pool.wait_ge(zeroed, 2)
            nc.gpsimd.memset(f32(q_ones), 1.0).then_inc(zeroed, 1)
            pool.wait_ge(zeroed, 3)
            nc.gpsimd.memset(f32(v_sb[:, :, :, :, 2 * DK:VCOLS]), 1.0).then_inc(zeroed, 1)
            pool.wait_ge(zeroed, 4)
            nc.gpsimd.memset(eps[:, :], LN_EPS).then_inc(zeroed, 1)
            pool.wait_ge(zeroed, 5)
            for n, (kind, m) in enumerate(FIRST):
                if n % 2 == 1:
                    split_lo(1, n // 2, kind, m, FIRST_AT[n])
            for it in items(pool):
                for g in range(UNITS):
                    v = it.i * UNITS + (g - 1)
                    pieces = pieces_of(it, g)
                    if g == 1 and not it.first:
                        add_bias(it)
                    if g == 3 and not it.first and not it.tail:
                        gamma_beta(it)
                    for step in ORDER[g]:
                        if not it.does(g, step):
                            continue
                        if step in LO_ON_POOL:
                            projection_lo(it, g, step)
                        elif step[0] == "X":
                            n = int(step[1:])
                            if not LO_ON_DVE[n]:
                                exponentials_lo(v, n)
                            if n in SPLIT_STEPS and pieces:
                                split_piece(it, pieces.pop(0))
                    for piece in pieces:
                        split_piece(it, piece)
                    if it.tail and g == 2:
                        gamma_beta(it)


def kernel(**inputs):
    import numpy as np
    import concourse.bacc as bacc
    from concourse.bass_utils import run_bass_kernel_spmd

    a = {name: np.asarray(value) for name, value in inputs.items()}
    x, ctx = a["x"], a["ctx_1024"]
    B, SQ, D = x.shape
    SKV = ctx.shape[1]
    P, KT, DK = 128, D // 128, D // HEADS

    def turned(t):
        return np.ascontiguousarray(t.reshape(t.shape[0], t.shape[1], KT, P).transpose(0, 3, 2, 1))

    def by_dim(w):
        return w.reshape(KT, GROUP, DK, -1).transpose(0, 2, 1, 3).reshape(KT, P, -1)

    def pieces(wq, wk, wv, wo):
        out = []
        for w in (wk, wq):
            out += [w_g.T.reshape(KT, P, P).transpose(1, 0, 2).reshape(P, -1) for w_g in by_dim(w)]
        for half in range(2):
            t = wv[half * D // 2:(half + 1) * D // 2].T.reshape(2, 2, P, D // 2)
            out += [t_k.transpose(1, 0, 2).reshape(P, -1) for t_k in t]
        out += list(by_dim(np.ascontiguousarray(wo.T)))
        return np.stack(out)

    wq, wk, wv = (a["L0_xattn_W_qkv"][n * D:(n + 1) * D] for n in range(3))
    bq, bk, bv = (a["L0_xattn_b_qkv"][n * D:(n + 1) * D] for n in range(3))
    w_pieces = np.stack([pieces(wq, wk, wv, a["L0_xattn_W_o"]),
                         pieces(*(a[f"L1_xattn_W{c}"] for c in "qkvo"))])
    cols = np.stack([np.stack([by_dim(b)[:, :, 0] for b in layer]) for layer in
                     ((bk, bq, bv), tuple(a[f"L1_xattn_b{c}"] for c in "kqv"))])
    rows = np.stack([np.stack([a["L0_xattn_b_o"], a["L0_xattn_ln_gamma"], a["L0_xattn_ln_beta"]]),
                     np.stack([a["L1_xattn_bo"], a["L1_xattn_gamma"], a["L1_xattn_beta"]])])
    arrays = {
        "x": np.ascontiguousarray(x),
        "x_t": turned(x),
        "ctx_t": turned(ctx),
        "w_pieces": np.ascontiguousarray(w_pieces),
        "bias_cols": np.ascontiguousarray(cols.transpose(3, 0, 1, 2)),
        "bias_rows": np.ascontiguousarray(np.broadcast_to(rows[:, None], (LAYERS, P, 3, D))),
        "identity": np.eye(P, dtype=np.float32),
    }
    nc = bacc.Bacc("TRN2", target_bir_lowering=False, num_devices=1)
    args = [nc.dram_tensor(f"in_{name}", t.shape, mybir.dt.from_np(t.dtype), kind="ExternalInput").ap()
            for name, t in arrays.items()]
    args.append(nc.dram_tensor("out", (B, SQ, D), F32, kind="ExternalOutput").ap())
    cross_attention_stack(nc, *args)
    r = run_bass_kernel_spmd(nc, [{f"in_{name}": t for name, t in arrays.items()}], core_ids=[0])
    return r.results[0]["out"]
```

```python
from contextlib import ExitStack

import concourse.bass as bass
from concourse import mybir

F32 = mybir.dt.float32
F32R = mybir.dt.float32r
ALU = mybir.AluOpType
ACT = mybir.ActivationFunctionType
AX = mybir.AxisListType

LAYERS = 2
HEADS = 16
GROUP = 4
UNITS = HEADS // GROUP
LN_EPS = 1e-5

ORDER = [steps.split() for steps in (
    "X0 Y9 M1 X1 Y10 X2 Y11 S0 X3 Y0 S1 V0 X4 Y1 S2 V1 X5 Y2 S3 K0 X6 Y3 M0 K1 S4 X7 Y4 Q S5 T0 X8 Y5 V2 S6 X9 Y6 S7 X10 Y7 X11 Y8 T1",
    "Y9 V0 M1 X0 X1 Y10 S0 Y11 V1 X2 S1 X3 Y0 X4 Y1 S2 K0 X5 Y2 S3 K1 X6 M0 Y3 Q S4 X7 Y4 V2 X8 S5 Y5 X9 X10 S6 Y6 Y7 X11 Y8 S7",
    "Y9 V0 M1 X0 X1 Y10 S0 Y11 V1 X2 S1 X3 Y0 X4 Y1 S2 K0 X5 Y2 S3 K1 X6 M0 Y3 Q S4 X7 Y4 V2 X8 S5 Y5 X9 X10 S6 Y6 Y7 X11 Y8 S7",
    "V0 X0 Y9 M1 X1 Y10 V1 S0 X2 Y11 V2 S1 X3 Y0 S2 K0 X4 Y1 S3 K1 X5 Y2 M0 Q X6 Y3 S4 O0 X7 Y4 S5 X8 Y5 O1 S6 X9 Y6 X10 Y7 X11 Y8 S7")]
LAG = 3
SPLIT_AT = [(4, 5, 9, 11), (8, 10, 11), (9, 10, 11), (6, 8, 10)]
NORM_AT = (5, 6, 7, 8, 9, 10)


def later(order, delays):
    at = [(n + (delays[step[0]] + 0.5 if delays.get(step[0]) else 0), step) for n, step in enumerate(order)]
    return [step for _, step in sorted(at, key=lambda pair: pair[0])]


DVE_DELAY = {'X': 2, 'K': 3, 'Q': 2, 'V': 2}
ACT_DELAY = {'K': 0, 'Q': 0, 'V': 0}
DVE_LO = (2, 6, 11)
ACT_HI = (1, 3, 4, 5, 6, 7, 8, 9, 11)
LN_AT = (0, 0)


def wait(engine, semaphore, count):
    if not isinstance(count, int) or count > 0:
        engine.wait_ge(semaphore, count)


def cross_attention_stack(nc, x, x_t, ctx_t, w_pieces, bias_cols, bias_rows, identity, out):
    B, SQ, D = x.shape
    P = 128
    KT = D // P
    SKV = ctx_t.shape[3]
    DK = D // HEADS
    KEYS = 125
    NKT = SKV // KEYS
    QH = SQ // 2
    SPAN = 376
    K_HALVES = [(0, SPAN), (SPAN, SKV)]
    ITEMS = LAYERS * B
    PAIRS = GROUP * NKT // 2
    PER_HEAD = NKT // 2
    PAIR = 2 * SQ
    SCALE = float(DK) ** -0.5
    VCOLS = 2 * DK + 1
    PIECE = 512
    assert D == KT * P and SKV == NKT * KEYS and DK * GROUP == P and PAIR <= 512 and 2 * SPAN >= SKV

    LO_ON_DVE = [c in DVE_LO for c in range(PAIRS)]
    N_LO_DVE = sum(LO_ON_DVE)
    N_LO_POOL = PAIRS - N_LO_DVE
    HI_ON_ACT = [c in ACT_HI for c in range(PAIRS)]
    N_HI_ACT = sum(HI_ON_ACT)
    N_HI_DVE = PAIRS - N_HI_ACT
    N_A = 6

    def ordinal(g, name):
        return [step for step in ACT_ORDER[g] if step[0] in "KQV"].index(name) + 1

    FIRST = [("c", 0), ("c", 1), ("c", 2), ("c", 3), ("v", 0), ("v", 1), ("k", 0), ("q", 0), ("x", 0), ("x", 1)]
    X_PIECES = [("x", 0), ("x", 1)]
    C_PIECES = [("c", 0), ("c", 1), ("c", 2), ("c", 3)]
    REST = {0: [("k", 1), ("q", 1)], 1: [("k", 2), ("q", 2), ("v", 2), ("v", 3)], 2: [("k", 3), ("q", 3)]}
    REFRESH = {0: [("k", 0), ("q", 0)], 1: [("k", 1), ("q", 1), ("v", 0), ("v", 1)], 2: [("k", 2), ("q", 2)]}
    OUTPUT = {1: [("o", 0), ("o", 1)], 2: [("o", 2), ("o", 3)]}
    WEIGHTS = {0: REST, 1: OUTPUT, B - 1: REFRESH, B: {1: [("v", 2), ("v", 3), ("k", 3), ("q", 3)]}, B + 1: OUTPUT}
    PIECE_INDEX = {**{("k", g): g for g in range(4)}, **{("q", g): 4 + g for g in range(4)},
                   **{("v", n): 8 + n for n in range(4)}, **{("o", k): 12 + k for k in range(4)}}

    x1 = nc.dram_tensor("x1", (B, SQ, D), F32, kind="Internal").ap()
    x1_t = nc.dram_tensor("x1_t", (B, P, KT, SQ), F32, kind="Internal").ap()

    DVE_ORDER = [later(order, DVE_DELAY) for order in ORDER]
    ACT_ORDER = [later(order, ACT_DELAY) for order in ORDER]

    class Item:

        def __init__(self, i, lo, pj0, raw0):
            self.i, self.lo = i, lo
            self.layer = 0 if lo < B else 1
            self.first = lo == 0
            self.tail = lo == ITEMS
            self.refresh = lo == B - 1
            self.out_layer = 0 if lo <= B else 1
            self.ends_layer0 = lo == B + 1
            self.pj0, self.raw0 = pj0, raw0

        def exists(self, g, lag):
            return not (self.first and g < lag) and not (self.tail and g >= lag)

        def does(self, g, step):
            if step[0] in "KQV":
                return not self.tail
            if step[0] == "S" or step == "M0":
                return self.exists(g, 1)
            if step == "M1":
                return self.exists(g, 2)
            if step[0] in "XY":
                return self.exists(g, 3 if step[0] == "Y" and int(step[1:]) >= PAIRS - LAG else 2)
            if step[0] == "O":
                return not self.first and g == 3
            return g == 0 and 2 <= self.lo < B + 2

        def groups(self, g):
            return [name for name in ORDER[g] if name[0] in "KQVOT" and self.does(g, name)]

        def n_groups(self):
            return sum(len(self.groups(g)) for g in range(UNITS))

        def pj(self, g, name):
            n = sum(len(self.groups(h)) for h in range(g)) + self.groups(g).index(name)
            return n % 2, self.pj0 + n // 2

        def n_raw(self):
            return sum(len(pieces_of(self, g)) for g in range(UNITS))

        def raw(self, n):
            return n % 2, self.raw0 + n // 2

    SEGMENTS = [(0, 1), (1, 2), (2, B - 1), (B - 1, B), (B, B + 1), (B + 1, B + 2), (B + 2, ITEMS - 1),
                (ITEMS - 1, ITEMS), (ITEMS, ITEMS + 1)]

    def items(engine):
        pj0, raw0 = 0, len(FIRST) // 2
        for lo, hi in SEGMENTS:
            probe = Item(lo, lo, 0, 0)
            assert probe.n_groups() % 2 == 0 and probe.n_raw() % 2 == 0
            n_pj, n_raw = probe.n_groups() // 2, probe.n_raw() // 2
            if hi - lo == 1:
                yield Item(lo, lo, pj0, raw0)
            else:
                with engine.Fori(lo, hi) as i:
                    yield Item(i, lo, i * n_pj + (pj0 - lo * n_pj), i * n_raw + (raw0 - lo * n_raw))
            pj0 += n_pj * (hi - lo)
            raw0 += n_raw * (hi - lo)

    def pieces_of(it, g):
        def in_slot(h):
            found = list(X_PIECES) if h == 0 and not it.first and not it.tail else []
            found += WEIGHTS.get(it.lo, {}).get(h, [])
            if h == 3 and it.lo < ITEMS - 1:
                found += C_PIECES
            return found
        at = sum(len(in_slot(h)) for h in range(g))
        return [(at + m, *piece) for m, piece in enumerate(in_slot(g))]

    with ExitStack() as stack:
        def sb(name, shape, dt=F32):
            return stack.enter_context(nc.sbuf_tensor(name, shape, dt))

        def psum(name, shape):
            return stack.enter_context(nc.psum_tensor(name, shape, F32))

        def sem(name):
            return stack.enter_context(nc.semaphore(name))

        w_hi = sb("w_hi", [P, 4, KT, D], F32R)
        w_lo = sb("w_lo", [P, 4, KT, D], F32R)
        c_hi = sb("c_hi", [P, KT, SKV], F32R)
        c_lo = sb("c_lo", [P, KT, SKV], F32R)
        x_hi = sb("x_hi", [P, KT, SQ], F32R)
        x_lo = sb("x_lo", [P, KT, SQ], F32R)
        raw = sb("raw", [P, 2, SKV])
        k_stack = sb("k_stack", [P, 2, GROUP, SKV], F32R)
        q_stack = sb("q_stack", [P, 2, GROUP, SQ], F32R)
        v_sb = sb("v_sb", [KEYS, 2, NKT, 2 * GROUP, VCOLS], F32R)
        e_ring = sb("e_ring", [P, 3, PAIR])
        e_hi = sb("e_hi", [KEYS, 4, PAIR], F32R)
        e_lo = sb("e_lo", [KEYS, 4, PAIR], F32R)
        e_flat = e_ring[:, :, :].rearrange("p a n -> p (a n)")
        stage = [sb("stage_hi", [P, SKV + SQ], F32R), sb("stage_lo", [P, SKV + SQ], F32R)]
        k_stage = [t[:, 0:SKV] for t in stage]
        q_stage = [t[:, SKV:SKV + SQ] for t in stage]
        row_max = sb("row_max", [P, 2, 2, 2])
        pv_sb = sb("pv_sb", [VCOLS, 2, PAIR])
        pv_wide = sb("pv_wide", [P, 3, SQ])
        a_hi = sb("a_hi", [P, UNITS, SQ], F32R)
        a_lo = sb("a_lo", [P, UNITS, SQ], F32R)
        y_sb = sb("y_sb", [P, 2, D])
        yt_sb = sb("yt_sb", [P, KT, QH])
        cols = sb("cols", [P, LAYERS, 3, UNITS])
        rows = sb("rows", [P, 3, D])
        ident = sb("ident", [P, P])
        eps = sb("eps", [P, 1])
        stats = sb("stats", [P, 2, 6])
        moments = sb("moments", [P, 2, 2])
        rstd = sb("rstd", [P, 6, 2])

        proj = psum("proj", [P, 2, 512])
        sc = psum("sc", [P, 4, 512])
        pv = psum("pv", [P, 2, 512])

        consts_loaded = sem("consts_loaded")
        rows_loaded = sem("rows_loaded")
        piece_loaded = {piece: sem("loaded_%s%d" % piece) for piece in list(PIECE_INDEX) + X_PIECES + C_PIECES}
        raw_hi = [sem(f"raw_hi{n}") for n in range(2)]
        raw_split = [sem(f"raw_split{n}") for n in range(2)]
        zeroed = sem("zeroed")
        selectors_loaded = sem("selectors_loaded")
        proj_ready = [sem(f"proj_ready{n}") for n in range(2)]
        hi_done = sem("hi_done")
        proj_taken = [sem(f"proj_taken{n}") for n in range(2)]
        stack_loaded = [sem(f"stack_loaded{n}") for n in range(2)]
        scores_ready = sem("scores_ready")
        max_done = sem("max_done")
        maxima_turned = sem("maxima_turned")
        maxima_placed = sem("maxima_placed")
        shifted_ready = sem("shifted_ready")
        exp_done = sem("exp_done")
        e_hi_act = sem("e_hi_act")
        e_hi_dve = sem("e_hi_dve")
        e_lo_dve = sem("e_lo_dve")
        e_lo_pool = sem("e_lo_pool")
        pv_done = sem("pv_done")
        pv_taken = sem("pv_taken")
        wide_loaded = sem("wide_loaded")
        norm_step = sem("norm_step")
        y_loaded = sem("y_loaded")
        y_biased = sem("y_biased")
        ln_step = sem("ln_step")
        ln_act = sem("ln_act")
        stats_seen = sem("stats_seen")
        normed = sem("normed")
        out_ready = sem("out_ready")
        out_stored = sem("out_stored")
        yt_stored = sem("yt_stored")

        block = stack.enter_context(nc.Block())

        STACK_DMAS = 6
        WIDE_DMAS = 6
        NORM_STEPS = 6
        LN_STEPS = 9
        LN_PARTS = 4
        f32 = lambda ap: ap.bitcast(F32)
        q_ones = stage[1][0:1, 0:SKV]

        def piece_columns(kind, n):
            return {"c": SKV, "x": 2 * SQ}.get(kind, PIECE)

        def piece_source(kind, n, item, layer):
            if kind == "c":
                return ctx_t[item - B if layer else item, :, n, :]
            if kind == "x":
                return (x1_t[item - B] if layer else x_t[item])[:, 2 * n:2 * n + 2, :]
            return w_pieces[layer, PIECE_INDEX[kind, n]]

        def piece_targets(kind, n):
            if kind == "c":
                return [t[:, n, :] for t in (c_hi, c_lo)]
            if kind == "x":
                return [t[:, 2 * n:2 * n + 2, :] for t in (x_hi, x_lo)]
            if kind in "kq":
                return [t[:, "kq".index(kind), :, n * P:(n + 1) * P] for t in (w_hi, w_lo)]
            if kind == "v":
                half, k = divmod(n, 2)
                return [t[:, 2, 2 * k:2 * k + 2, half * 2 * P:(half + 1) * 2 * P] for t in (w_hi, w_lo)]
            return [t[:, 3, n, :] for t in (w_hi, w_lo)]

        def flat(t):
            return t[:, :, :].rearrange("p a n -> p (a n)")

        FIRST_AT = [raw[:, 0, :], raw[:, 1, :], e_flat[:, 0:SKV], flat(rows)[:, 0:SKV], y_sb[:, 0, :], y_sb[:, 1, :],
                    flat(rows)[:, SKV:SKV + PIECE], flat(pv_wide)[:, 0:PIECE], flat(yt_sb), e_flat[:, SKV:SKV + 2 * SQ]]

        def piece_raw(kind, n, place):
            if kind == "c" or kind == "o":
                return place
            return place.rearrange("p (a n) -> p a n", a=4 if kind in "kq" else 2)

        def raw_slot(it, n, kind):
            return raw[:, it.raw(n)[0], 0:piece_columns(kind, n)]

        def last_reader(it, g, kind):
            return it.pj(g, {"v": "V2", "k": "K1", "c": "K1"}.get(kind, "Q"))

        def hi_ready(engine, v, c):
            v, c = (v, c) if c >= 0 else (v - 1, c + PAIRS)
            n = sum(HI_ON_ACT[:c + 1])
            if HI_ON_ACT[c]:
                wait(engine, e_hi_act, v * N_HI_ACT + n)
            else:
                wait(engine, e_hi_dve, v * N_HI_DVE + c + 1 - n)

        def lo_ready(engine, v, c):
            v, c = (v, c) if c >= 0 else (v - 1, c + PAIRS)
            n = sum(LO_ON_DVE[:c + 1])
            if LO_ON_DVE[c]:
                wait(engine, e_lo_dve, v * N_LO_DVE + n)
            else:
                wait(engine, e_lo_pool, v * N_LO_POOL + c + 1 - n)


        @block.sync
        def _(sp):
            sp.dma_start(cols[:, :, :, :], bias_cols).then_inc(consts_loaded, 16)
            sp.dma_start(ident[:, :], identity).then_inc(consts_loaded, 16)

            def load(kind, m, place, item, layer):
                sp.dma_start(piece_raw(kind, m, place), piece_source(kind, m, item, layer)).then_inc(piece_loaded[kind, m], 16)

            for n, (kind, m) in enumerate(FIRST):
                load(kind, m, FIRST_AT[n], 0, 0)
            sp.wait_ge(zeroed, 3)
            for b in range(2):
                for j in range(GROUP):
                    r = 3 * DK + j % 2
                    sp.dma_start(f32(k_stack[r:r + 1, b, j, :]), f32(q_ones)).then_inc(selectors_loaded, 16)

            def store_result(it, count):
                sp.wait_ge(out_ready, count)
                dst = out[it.i - 2 - B] if it.lo > B + 1 else x1[it.i - 2]
                for t in range(2):
                    sp.dma_start(dst[t * QH:(t + 1) * QH, :], y_sb[0:QH, t, :]).then_inc(out_stored, 16)
                if it.ends_layer0:
                    sp.dma_start(rows[:, :, :], bias_rows[1]).then_inc(rows_loaded, 16)

            for turn in range(2):
                sp.wait_ge(raw_split[turn], len(FIRST) // 2)
            sp.dma_start(rows[:, :, :], bias_rows[0]).then_inc(rows_loaded, 16)

            def load_stack(b, pair):
                heads, of = slice(2 * pair, 2 * pair + 2), slice(2 * DK * pair, 2 * DK * (pair + 1))
                for r, part in ((0, 0), (DK, 0), (2 * DK, 1)):
                    sp.dma_start(f32(k_stack[r:r + DK, b, heads, :]), f32(k_stage[part][of, :])).then_inc(stack_loaded[pair], 16)
                for r, part in ((0, 0), (DK, 1), (2 * DK, 0)):
                    sp.dma_start(f32(q_stack[r:r + DK, b, heads, :]), f32(q_stage[part][of, :])).then_inc(stack_loaded[pair], 16)

            for it in items(sp):
                value = (lambda v: v) if isinstance(it.i, int) else sp.snap
                left = {g: value(it.i * (N_LO_DVE * UNITS) + (g - 2) * N_LO_DVE) for g in range(UNITS) if it.exists(g, 3)}
                if not it.tail:
                    taken = [value(it.pj(g, "Q")[1] + 1) for g in range(UNITS)]
                    free = [value(it.raw(n)[1]) for n in range(it.n_raw())]
                pv_count = [value(it.i * (2 * UNITS) + 2 * (g - 2)) for g in range(UNITS)]
                twice = value(it.i * 2 - 2)
                turned = {t: value(it.pj(0, f"T{t}")[1] + 1) for t in range(2) if it.does(0, f"T{t}")}
                stored = value(it.i * 32 - 32)
                for g in range(UNITS):
                    b = g % 2
                    if g == 2 and not it.first:
                        wait(sp, out_stored, stored)
                        src = x1[it.i - (B + 1)] if it.out_layer else x[it.i - 1]
                        sp.dma_start(y_sb[0:QH, :, :], src.rearrange("(t q) d -> q t d", q=QH)).then_inc(y_loaded, 16)
                    pieces = pieces_of(it, g)

                    def load_pieces(some):
                        for n, kind, m in some:
                            item, layer = (it.i, it.layer) if kind == "x" else (it.i + 1, int(it.lo >= B - 1))
                            sp.wait_ge(raw_split[it.raw(n)[0]], free[n])
                            load(kind, m, raw_slot(it, n, kind), item, layer)

                    load_pieces(pieces[:2])
                    if it.exists(g, 1):
                        if it.exists(g, 3):
                            sp.wait_ge(e_lo_dve, left[g])
                        load_stack((g + 1) % 2, 1)
                    if it.exists(g, 3):
                        sp.wait_ge(pv_taken, pv_count[g])
                        for part in range(2):
                            src = pv_sb[part * DK:(part + 1) * DK, :, :].rearrange("d a (b q) -> d (a b) q", b=2)
                            sp.dma_start(pv_wide[:, part, :], src).then_inc(wide_loaded, 16)
                        for j in range(GROUP):
                            one = pv_sb[2 * DK:2 * DK + 1, :, :]
                            src = bass.AP(one.tensor, one.offset + j * SQ, [[2 * PAIR, 1], [0, DK], [1, SQ]])
                            sp.dma_start(pv_wide[j:P:GROUP, 2, :], src).then_inc(wide_loaded, 16)

                    def store_turned(t):
                        if g == 0 and t in turned:
                            sp.wait_ge(proj_taken[it.pj(g, f"T{t}")[0]], turned[t])
                            sp.dma_start(x1_t[it.i - 2, :, :, t * QH:(t + 1) * QH], yt_sb[:, :, :]).then_inc(yt_stored, 16)

                    if not it.tail:
                        sp.wait_ge(proj_taken[it.pj(g, "Q")[0]], taken[g])
                        load_stack(g % 2, 0)
                    load_pieces(pieces[2:4])
                    store_turned(0)
                    load_pieces(pieces[4:])
                    if g == 0 and it.lo >= 2:
                        store_result(it, twice)
                    store_turned(1)
                if it.tail:
                    store_result(Item(ITEMS + 1, ITEMS + 1, 0, 0), 2 * ITEMS)
            sp.wait_ge(out_stored, 32 * ITEMS)
            sp.wait_ge(yt_stored, 32 * B)

        @block.tensor
        def _(pe):
            def free_bank(it, g, name):
                bank, k = it.pj(g, name)
                wait(pe, proj_taken[bank], k)
                return bank

            def three_passes(target, w, w2, a, a2, k):
                nc.tensor.matmul(target, w, a, start=(k == 0), stop=False)
                nc.tensor.matmul(target, w2, a, start=False, stop=False)
                return nc.tensor.matmul(target, w, a2, start=False, stop=(k == KT - 1))

            def first_split(it, n):
                if it.first:
                    pe.wait_ge(raw_split[n % 2], n // 2 + 1)
                    pe.wait_ge(raw_split[1 - n % 2], (n + 1) // 2)

            def weights_split(it, g):
                n = max([n for h in range(g) for n, kind, _ in pieces_of(it, h) if kind in "kqvo"])
                for turn in range(2):
                    pe.wait_ge(raw_split[turn], it.raw0 + (n + 2 - turn) // 2)

            def project_keys(it, g, half):
                first_split(it, [6, 10, 12, 16][g])
                lo, hi = K_HALVES[half]
                bank = free_bank(it, g, f"K{half}")
                for k in range(KT):
                    cs = slice(g * P, (g + 1) * P)
                    mm = three_passes(proj[:, bank, 0:hi - lo], w_hi[:, 0, k, cs], w_lo[:, 0, k, cs],
                                      c_hi[:, k, lo:hi], c_lo[:, k, lo:hi], k)
                mm.then_inc(proj_ready[bank], 1)

            def project_queries(it, g):
                first_split(it, [9, 11, 13, 17][g])
                if not it.first and g == 0:
                    for slot in range(2):
                        pe.wait_ge(raw_split[slot], it.raw0 + 1)
                bank = free_bank(it, g, "Q")
                for k in range(KT):
                    cs = slice(g * P, (g + 1) * P)
                    mm = three_passes(proj[:, bank, 0:SQ], w_hi[:, 1, k, cs], w_lo[:, 1, k, cs],
                                      x_hi[:, k, :], x_lo[:, k, :], k)
                mm.then_inc(proj_ready[bank], 1)

            def project_values(it, g, n):
                first_split(it, [5, 5, 15, 15][g])
                if not it.first and g == 0 and n == 0:
                    for slot in range(2):
                        pe.wait_ge(raw_split[slot], it.raw0)
                half, kt = g // 2, 3 * (g % 2) + n
                if it.lo == B and g == 2 and n == 0:
                    weights_split(it, g)
                bank = free_bank(it, g, f"V{n}")
                ks = slice(kt * KEYS, (kt + 1) * KEYS)
                ds = slice(half * 2 * P, (half + 1) * 2 * P)
                for k in range(KT):
                    mm = three_passes(proj[0:KEYS, bank, 0:2 * P], c_hi[:, k, ks], c_lo[:, k, ks],
                                      w_hi[:, 2, k, ds], w_lo[:, 2, k, ds], k)
                mm.then_inc(proj_ready[bank], 1)

            def scores(v, t, b):
                j, qt = divmod(t, 2)
                wait(pe, max_done, v * (2 * GROUP) + t)
                if t % GROUP == 0:
                    wait(pe, maxima_placed, v * 2 + t // GROUP)
                q = q_stack[0:3 * DK, b, j, qt * QH:(qt + 1) * QH]
                nc.tensor.matmul(sc[0:QH, 0, 0:SPAN], q, k_stack[0:3 * DK, b, j, 0:SPAN], start=True, stop=True)
                nc.tensor.matmul(sc[0:QH, 1, 0:SPAN], q, k_stack[0:3 * DK, b, j, SKV - SPAN:SKV],
                                 start=True, stop=True).then_inc(scores_ready, 1)

            def turn_maxima(v, pair):
                pe.wait_ge(max_done, v * (2 * GROUP) + 4 * (pair + 1))
                for qt in range(2):
                    mm = nc.tensor.transpose(sc[0:2, qt, SPAN:SPAN + QH], row_max[0:QH, pair, qt, :], ident[0:QH, 0:QH])
                mm.then_inc(maxima_turned, 1)

            def shifted_scores(v, c, b):
                j, m = divmod(c, PER_HEAD)
                if c in (0, 2 * PER_HEAD):
                    pe.wait_ge(maxima_placed, v * 2 + 1 + c // (2 * PER_HEAD))
                wait(pe, exp_done, v * PAIRS + (c - 1))
                for n in range(2):
                    ks = slice((2 * m + n) * KEYS, (2 * m + n + 1) * KEYS)
                    mm = nc.tensor.matmul(sc[0:KEYS, 2 + c % 2, n * SQ:(n + 1) * SQ], k_stack[:, b, j, ks],
                                          q_stack[:, b, j, :], start=True, stop=True)
                mm.then_inc(shifted_ready, 1)

            def times_values(v, c, gv):
                j, m = divmod(c, PER_HEAD)
                if c in (0, 2 * PER_HEAD):
                    wait(pe, pv_taken, v * 2 - 1 + c // (2 * PER_HEAD))
                hi_ready(pe, v, c)
                lo_ready(pe, v, c)
                for n in range(2):
                    kt = 2 * m + n
                    target = pv[0:VCOLS, j // 2, (j % 2) * SQ:(j % 2 + 1) * SQ]
                    values = v_sb[:, gv // 2, kt, GROUP * (gv % 2) + j, :]
                    nc.tensor.matmul(target, values, e_hi[0:KEYS, c % 4, n * SQ:(n + 1) * SQ], start=(kt == 0), stop=False)
                    mm = nc.tensor.matmul(target, values, e_lo[0:KEYS, c % 4, n * SQ:(n + 1) * SQ],
                                          start=False, stop=(kt == NKT - 1))
                mm.then_inc(pv_done, 1)

            def project_out(it, g, t):
                bank = free_bank(it, g, f"O{t}")
                if it.lo in (1, B + 1) and t == 0:
                    weights_split(it, g)
                pe.wait_ge(norm_step, it.i * (UNITS * NORM_STEPS))
                qs = slice(t * QH, (t + 1) * QH)
                for k in range(KT):
                    mm = three_passes(proj[0:QH, bank, 0:D], a_hi[:, k, qs], a_lo[:, k, qs],
                                      w_hi[:, 3, k, :], w_lo[:, 3, k, :], k)
                mm.then_inc(proj_ready[bank], 1)

            def turn_output(it, g, t):
                bank = free_bank(it, g, f"T{t}")
                pe.wait_ge(out_ready, it.i * 2 - 3 + t)
                for k in range(KT):
                    mm = nc.tensor.transpose(proj[:, bank, k * QH:(k + 1) * QH], y_sb[0:QH, t, k * P:(k + 1) * P],
                                             ident[0:QH, 0:QH])
                mm.then_inc(proj_ready[bank], 1)

            pe.wait_ge(consts_loaded, 32)
            for it in items(pe):
                for g in range(UNITS):
                    u = it.i * UNITS + g
                    b = (g + 1) % 2
                    for step in ORDER[g]:
                        if not it.does(g, step):
                            continue
                        n = int(step[1:] or 0)
                        if step in ("S0", "S4"):
                            pe.wait_ge(stack_loaded[n // GROUP], u * (16 * STACK_DMAS))
                        if step[0] == "S":
                            scores(u - 1, n, b)
                        elif step[0] == "M":
                            turn_maxima(u - 1 - n, n)
                        elif step[0] == "X":
                            if it.first and g == 2 and n == 0:
                                pe.wait_ge(zeroed, 5)
                                pe.wait_ge(selectors_loaded, 16 * 2 * GROUP)
                            shifted_scores(u - 2, n, g % 2)
                        elif step[0] == "Y":
                            lag = 2 if n < PAIRS - LAG else 3
                            times_values(u - lag, n, (g - lag) % UNITS)
                        elif step[0] == "K":
                            project_keys(it, g, n)
                        elif step[0] == "Q":
                            project_queries(it, g)
                        elif step[0] == "V":
                            project_values(it, g, n)
                        elif step[0] == "O":
                            project_out(it, g, n)
                        else:
                            turn_output(it, g, n)

        @block.scalar
        def _(act):
            act.preload_act_table_set("natural_log_exp_and_others")

            def split_hi(turn, count, kind, m, place):
                act.wait_ge(piece_loaded[kind, m], count)
                nc.scalar.activation(piece_targets(kind, m)[0], piece_raw(kind, m, place), ACT.Copy).then_inc(raw_hi[turn], 1)

            def split_piece(it, g, piece):
                n, kind, m = piece
                if kind == "c" or (it.refresh and kind != "x"):
                    bank, k = last_reader(it, g, kind)
                    act.wait_ge(proj_ready[bank], k + 1)
                count = it.i * 16 + (32 if kind == "c" else 16) if kind in "cx" else 16 * (1 + (it.lo >= B - 1))
                split_hi(it.raw(n)[0], count, kind, m, raw_slot(it, n, kind))

            def evacuate(it, g, name):
                bank, k = it.pj(g, name)
                act.wait_ge(proj_ready[bank], k + 1)
                bias = 0.0
                if name[0] == "V":
                    hi = v_sb[:, g // 2, 3 * (g % 2) + int(name[1]), :, 0:DK]
                    src = proj[0:KEYS, bank, 0:2 * P].rearrange("p (h d) -> p h d", d=DK)
                elif name == "Q":
                    hi, src, bias = q_stage[0], proj[:, bank, 0:SQ], cols[:, it.layer, 1, g:g + 1]
                else:
                    a, z = K_HALVES[int(name[1])]
                    hi, src, bias = k_stage[0][:, a:z], proj[:, bank, 0:z - a], cols[:, it.layer, 0, g:g + 1]
                if name == "K0" and not (it.first and g == 0):
                    for pair in range(2):
                        act.wait_ge(stack_loaded[pair], (it.i * UNITS + g) * (16 * STACK_DMAS))
                nc.scalar.activation(hi, src, ACT.Identity, bias=bias).then_inc(hi_done, 1)

            def maxima_rows(v, pair, b):
                act.wait_ge(maxima_turned, v * 2 + (pair + 1))
                turned = sc[0:2, 0:2, SPAN:SPAN + QH].unsqueeze(1).broadcast_to([2, 2, 2, QH])
                rows_of = q_stack[3 * DK:3 * DK + 2, b, 2 * pair:2 * pair + 2, :].rearrange("r j (t q) -> r j t q", q=QH)
                nc.scalar.activation(rows_of, turned, ACT.Copy, scale=-1.0).then_inc(maxima_placed, 1)

            def exponentials(v, c):
                act.wait_ge(shifted_ready, v * PAIRS + (c + 1))
                src = sc[0:KEYS, 2 + c % 2, 0:PAIR]
                if HI_ON_ACT[c]:
                    wait(act, pv_done, v * PAIRS + (c - 3))
                    nc.scalar.activation(e_hi[:, c % 4, :], src, ACT.Exp, scale=SCALE).then_inc(e_hi_act, 1)
                hi_ready(act, v, c - 3)
                lo_ready(act, v, c - 3)
                nc.scalar.activation(e_ring[0:KEYS, c % 3, :], src, ACT.Exp, scale=SCALE).then_inc(exp_done, 1)

            def take_products(v, n):
                act.wait_ge(pv_done, v * PAIRS + 2 * PER_HEAD * (n + 1))
                wait(act, wide_loaded, v * (16 * WIDE_DMAS))
                nc.scalar.activation(pv_sb[:, n, :], pv[0:VCOLS, n, 0:PAIR], ACT.Copy).then_inc(pv_taken, 1)

            def deviation(i):
                act.wait_ge(ln_step, i * LN_STEPS - (2 * LN_STEPS - 4))
                nc.scalar.activation(rstd[0:QH, 0, :], moments[0:QH, :, 1], ACT.Ln, bias=eps[0:QH, :]).then_inc(ln_act, 1)
                act.wait_ge(ln_act, i * 2 - 3)
                nc.scalar.activation(rstd[0:QH, 1, :], rstd[0:QH, 0, :], ACT.Exp, scale=-0.5).then_inc(ln_act, 1)

            for n, (kind, m) in enumerate(FIRST):
                split_hi(n % 2, 16, kind, m, FIRST_AT[n])
            act.wait_ge(consts_loaded, 32)
            act.wait_ge(selectors_loaded, 16 * 2 * GROUP)
            for it in items(act):
                for g in range(UNITS):
                    u = it.i * UNITS + g
                    b = (g + 1) % 2
                    pieces = pieces_of(it, g)
                    for step in ACT_ORDER[g]:
                        if not it.does(g, step):
                            continue
                        n = int(step[1:] or 0)
                        if step[0] in "KQV":
                            evacuate(it, g, step)
                        elif step == "Y11":
                            take_products(u - 3, 1)
                        elif step[0] == "M":
                            maxima_rows(u - 1 - n, n, (g + 1 + n) % 2)
                        elif step[0] == "T":
                            bank, k = it.pj(g, step)
                            act.wait_ge(proj_ready[bank], k + 1)
                            wait(act, yt_stored, it.i * 32 - (64 - 16 * n))
                            nc.scalar.activation(yt_sb[:, :, :], proj[:, bank, 0:KT * QH].rearrange("p (k q) -> p k q", q=QH),
                                                 ACT.Copy).then_inc(proj_taken[bank], 1)
                        elif step[0] == "X":
                            exponentials(u - 2, n)
                            if n == LN_AT[0] and g == 0 and it.lo >= 2:
                                deviation(it.i)
                            if n == 9:
                                take_products(u - 2, 0)
                            if n in SPLIT_AT[g] and pieces:
                                split_piece(it, g, pieces.pop(0))
                    for piece in pieces:
                        split_piece(it, g, piece)
                    if it.tail and g == 3:
                        deviation(it.i + 1)

        @block.vector
        def _(dve):
            def split_lo(turn, k, kind, m, place):
                dve.wait_ge(raw_hi[turn], k + 1)
                hi, lo = piece_targets(kind, m)
                nc.vector.tensor_tensor(lo, piece_raw(kind, m, place), f32(hi), ALU.subtract).then_inc(raw_split[turn], 1)

            def split_piece(it, piece):
                n, kind, m = piece
                if it.raw(n)[0] == 0:
                    split_lo(*it.raw(n), kind, m, raw_slot(it, n, kind))

            def row_maxima(v, t):
                j, qt = divmod(t, 2)
                dve.wait_ge(scores_ready, v * (2 * GROUP) + (t + 1))
                nc.vector.tensor_reduce(row_max[0:QH, j // 2, qt, j % 2:j % 2 + 1], sc[0:QH, 0:2, 0:SPAN],
                                        AX.XY, ALU.max).then_inc(max_done, 1)

            def projection_lo(it, g, name):
                bank, k = it.pj(g, name)
                dve.wait_ge(hi_done, it.i * (N_A * UNITS) + (N_A * g + ordinal(g, name)))
                if name[0] == "V":
                    kt = 3 * (g % 2) + int(name[1])
                    op = nc.vector.tensor_tensor(v_sb[:, g // 2, kt, :, DK:2 * DK],
                                                 proj[0:KEYS, bank, 0:2 * P].rearrange("p (h d) -> p h d", d=DK),
                                                 f32(v_sb[:, g // 2, kt, :, 0:DK]), ALU.subtract)
                else:
                    if name == "Q":
                        (hi, lo), src, bias = q_stage, proj[:, bank, 0:SQ], cols[:, it.layer, 1, g:g + 1]
                    else:
                        a, z = K_HALVES[int(name[1])]
                        hi, lo = (t[:, a:z] for t in k_stage)
                        src, bias = proj[:, bank, 0:z - a], cols[:, it.layer, 0, g:g + 1]
                    op = nc.vector.scalar_tensor_tensor(out=lo, in0=src, scalar=bias, in1=f32(hi), op0=ALU.add,
                                                        op1=ALU.subtract)
                op.then_inc(proj_taken[bank], 1)

            def halves(v, c):
                ring, at = e_ring[0:KEYS, c % 3, :], c % 4
                if not (HI_ON_ACT[c] and not LO_ON_DVE[c]):
                    dve.wait_ge(exp_done, v * PAIRS + (c + 1))
                    wait(dve, pv_done, v * PAIRS + (c - 3))
                if not HI_ON_ACT[c]:
                    nc.vector.tensor_copy(e_hi[:, at, :], ring).then_inc(e_hi_dve, 1)
                if LO_ON_DVE[c]:
                    hi_ready(dve, v, c)
                    nc.vector.tensor_tensor(e_lo[:, at, :], ring, f32(e_hi[:, at, :]), ALU.subtract).then_inc(e_lo_dve, 1)

            def normalise(it, g, part):
                w = it.i * UNITS + (g - 3)
                gw = (g - 3) % UNITS
                bias = cols[:, it.layer if g >= 3 else it.out_layer, 2, gw:gw + 1]
                if part > 2:
                    dve.wait_ge(norm_step, w * NORM_STEPS + part)
                if part < 2:
                    if part == 0:
                        dve.wait_ge(wide_loaded, w * (16 * WIDE_DMAS) + 16 * WIDE_DMAS)
                    half = pv_wide[:, 2, part * QH:(part + 1) * QH]
                    op = nc.vector.reciprocal(half, half)
                elif part == 2:
                    op = nc.vector.tensor_tensor(pv_wide[:, 0, :], pv_wide[:, 0, :], pv_wide[:, 1, :], ALU.add)
                elif part == 3:
                    op = nc.vector.tensor_tensor(pv_wide[:, 0, :], pv_wide[:, 0, :], pv_wide[:, 2, :], ALU.mult)
                elif part == 4:
                    op = nc.vector.tensor_scalar(a_hi[:, gw, :], pv_wide[:, 0, :], bias, None, ALU.add)
                else:
                    op = nc.vector.scalar_tensor_tensor(out=a_lo[:, gw, :], in0=pv_wide[:, 0, :], scalar=bias,
                                                        in1=f32(a_hi[:, gw, :]), op0=ALU.add, op1=ALU.subtract)
                op.then_inc(norm_step, 1)

            def add_residual(it, g, t):
                dve.wait_ge(y_biased, it.i * 2 - 1 + t)
                step = it.i * LN_STEPS - LN_STEPS
                bank, k = it.pj(g, f"O{t}")
                dve.wait_ge(proj_ready[bank], k + 1)
                nc.vector.tensor_tensor(y_sb[0:QH, t, :], proj[0:QH, bank, 0:D], y_sb[0:QH, t, :],
                                        ALU.add).then_inc(proj_taken[bank], 1)
                dve.wait_ge(proj_taken[bank], k + 1)
                nc.vector.bn_stats(stats[0:QH, t, :], y_sb[0:QH, t, :]).then_inc(ln_step, 1)
                dve.wait_ge(ln_step, step + (2 * t + 1))
                dve.sem_inc(stats_seen, 1)
                nc.vector.bn_aggr(moments[0:QH, t, :], stats[0:QH, t:t + 1, :]).then_inc(ln_step, 1)

            def layer_norm(i, part):
                step = i * LN_STEPS - 2 * LN_STEPS
                r = [rstd[0:QH, n, :] for n in range(6)]
                if part == 0:
                    dve.wait_ge(ln_step, step + 4)
                    for t in range(2):
                        nc.vector.scalar_tensor_tensor(out=y_sb[0:QH, t, :], in0=y_sb[0:QH, t, :], scalar=moments[0:QH, t, 0:1],
                                                       in1=rows[0:QH, 1, :], op0=ALU.subtract, op1=ALU.mult).then_inc(normed, 1)
                    nc.vector.tensor_scalar(r[2], moments[0:QH, :, 1], LN_EPS, None, ALU.add).then_inc(ln_step, 1)
                elif part == 1:
                    dve.wait_ge(ln_act, i * 2 - 2)
                    nc.vector.tensor_tensor(r[3], r[1], r[1], ALU.mult).then_inc(ln_step, 1)
                    dve.wait_ge(ln_step, step + 6)
                    nc.vector.tensor_tensor(r[4], r[3], r[2], ALU.mult).then_inc(ln_step, 1)
                elif part == 2:
                    dve.wait_ge(ln_step, step + 7)
                    nc.vector.tensor_scalar(r[5], r[4], -0.5, 1.5, ALU.mult, ALU.add).then_inc(ln_step, 1)
                    dve.wait_ge(ln_step, step + 8)
                    nc.vector.tensor_tensor(r[0], r[1], r[5], ALU.mult).then_inc(ln_step, 1)
                else:
                    dve.wait_ge(ln_step, step + 9)
                    dve.wait_ge(normed, i * 2 - 2)
                    for t in range(2):
                        nc.vector.scalar_tensor_tensor(out=y_sb[0:QH, t, :], in0=y_sb[0:QH, t, :], scalar=rstd[0:QH, 0, t:t + 1],
                                                       in1=rows[0:QH, 2, :], op0=ALU.mult, op1=ALU.add).then_inc(out_ready, 1)

            dve.wait_ge(consts_loaded, 32)
            for n, (kind, m) in enumerate(FIRST):
                if n % 2 == 0:
                    split_lo(0, n // 2, kind, m, FIRST_AT[n])
            for it in items(dve):
                for g in range(UNITS):
                    u = it.i * UNITS + g
                    pieces = pieces_of(it, g)
                    for step in DVE_ORDER[g]:
                        if not it.does(g, step):
                            continue
                        n = int(step[1:] or 0)
                        if step[0] == "S":
                            row_maxima(u - 1, n)
                        elif step[0] in "KQV":
                            projection_lo(it, g, step)
                        elif step[0] == "O":
                            add_residual(it, g, n)
                        elif step[0] == "X":
                            halves(u - 2, n)
                            if n in NORM_AT and it.exists(g, 3):
                                normalise(it, g, NORM_AT.index(n))
                            if 0 <= n - LN_AT[1] < LN_PARTS and g == 0 and it.lo >= 2:
                                layer_norm(it.i, n - LN_AT[1])
                            if n in SPLIT_AT[g] and pieces:
                                split_piece(it, pieces.pop(0))
                    for piece in pieces:
                        split_piece(it, piece)
                    if it.tail and g == 2:
                        for part in range(NORM_STEPS):
                            normalise(it, g, part)
                    if it.tail and g == 3:
                        for part in range(LN_PARTS):
                            layer_norm(it.i + 1, part)

        @block.gpsimd
        def _(pool):
            def split_lo(turn, k, kind, m, place):
                pool.wait_ge(raw_hi[turn], k + 1)
                hi, lo = piece_targets(kind, m)
                nc.gpsimd.tensor_tensor(lo, piece_raw(kind, m, place), f32(hi), ALU.subtract).then_inc(raw_split[turn], 1)

            def split_piece(it, piece):
                n, kind, m = piece
                if it.raw(n)[0] == 1:
                    split_lo(*it.raw(n), kind, m, raw_slot(it, n, kind))

            def exponentials_lo(v, c):
                hi_ready(pool, v, c)
                pool.wait_ge(exp_done, v * PAIRS + (c + 1))
                wait(pool, pv_done, v * PAIRS + (c - 3))
                nc.gpsimd.tensor_tensor(e_lo[:, c % 4, :], e_ring[0:KEYS, c % 3, :], f32(e_hi[:, c % 4, :]),
                                        ALU.subtract).then_inc(e_lo_pool, 1)

            def add_bias(it):
                pool.wait_ge(rows_loaded, 32 if it.out_layer else 16)
                pool.wait_ge(y_loaded, it.i * 16)
                for t in range(2):
                    nc.gpsimd.tensor_tensor(y_sb[0:QH, t, :], y_sb[0:QH, t, :], rows[0:QH, 0, :], ALU.add).then_inc(y_biased, 1)

            nc.gpsimd.memset(f32(k_stack[3 * DK:P, :, :, :]), 0.0).then_inc(zeroed, 1)
            pool.wait_ge(zeroed, 1)
            nc.gpsimd.memset(f32(q_stack[3 * DK:P, :, :, :]), 0.0).then_inc(zeroed, 1)
            pool.wait_ge(zeroed, 2)
            nc.gpsimd.memset(f32(q_ones), 1.0).then_inc(zeroed, 1)
            pool.wait_ge(zeroed, 3)
            for n, (kind, m) in enumerate(FIRST):
                if n % 2 == 1:
                    split_lo(1, n // 2, kind, m, FIRST_AT[n])
            nc.gpsimd.memset(f32(v_sb[:, :, :, :, 2 * DK:VCOLS]), 1.0).then_inc(zeroed, 1)
            pool.wait_ge(zeroed, 4)
            nc.gpsimd.memset(eps[:, :], LN_EPS).then_inc(zeroed, 1)
            for it in items(pool):
                for g in range(UNITS):
                    u = it.i * UNITS + g
                    pieces = pieces_of(it, g)
                    if g == 3 and not it.first:
                        add_bias(it)
                    for step in ORDER[g]:
                        if step[0] != "X" or not it.does(g, step):
                            continue
                        n = int(step[1:])
                        if not LO_ON_DVE[n]:
                            exponentials_lo(u - 2, n)
                        if n in SPLIT_AT[g] and pieces:
                            split_piece(it, pieces.pop(0))
                    for piece in pieces:
                        split_piece(it, piece)


def kernel(**inputs):
    import numpy as np
    import concourse.bacc as bacc
    from concourse.bass_utils import run_bass_kernel_spmd

    a = {name: np.asarray(value) for name, value in inputs.items()}
    x, ctx = a["x"], a["ctx_1024"]
    B, SQ, D = x.shape
    SKV = ctx.shape[1]
    P, KT, DK = 128, D // 128, D // HEADS

    def turned(t):
        return np.ascontiguousarray(t.reshape(t.shape[0], t.shape[1], KT, P).transpose(0, 3, 2, 1))

    def by_dim(w):
        return w.reshape(KT, GROUP, DK, -1).transpose(0, 2, 1, 3).reshape(KT, P, -1)

    def by_pair(w):
        return w.reshape(KT, 2, 2, DK, -1).transpose(0, 1, 3, 2, 4).reshape(KT, P, -1)

    def pieces(wq, wk, wv, wo):
        out = []
        for w in (wk, wq):
            out += [w_g.T.reshape(KT, P, P).transpose(1, 0, 2).reshape(P, -1) for w_g in by_pair(w)]
        for half in range(2):
            t = wv[half * D // 2:(half + 1) * D // 2].T.reshape(2, 2, P, D // 2)
            out += [t_k.transpose(1, 0, 2).reshape(P, -1) for t_k in t]
        out += list(by_dim(np.ascontiguousarray(wo.T)))
        return np.stack(out)

    wq, wk, wv = (a["L0_xattn_W_qkv"][n * D:(n + 1) * D] for n in range(3))
    bq, bk, bv = (a["L0_xattn_b_qkv"][n * D:(n + 1) * D] for n in range(3))
    w_pieces = np.stack([pieces(wq, wk, wv, a["L0_xattn_W_o"]),
                         pieces(*(a[f"L1_xattn_W{c}"] for c in "qkvo"))])
    cols = np.stack([np.stack([by(b)[:, :, 0] for by, b in zip((by_pair, by_pair, by_dim), layer)]) for layer in
                     ((bk, bq, bv), tuple(a[f"L1_xattn_b{c}"] for c in "kqv"))])
    rows = np.stack([np.stack([a["L0_xattn_b_o"], a["L0_xattn_ln_gamma"], a["L0_xattn_ln_beta"]]),
                     np.stack([a["L1_xattn_bo"], a["L1_xattn_gamma"], a["L1_xattn_beta"]])])
    arrays = {
        "x": np.ascontiguousarray(x),
        "x_t": turned(x),
        "ctx_t": turned(ctx),
        "w_pieces": np.ascontiguousarray(w_pieces),
        "bias_cols": np.ascontiguousarray(cols.transpose(3, 0, 1, 2)),
        "bias_rows": np.ascontiguousarray(np.broadcast_to(rows[:, None], (LAYERS, P, 3, D))),
        "identity": np.eye(P, dtype=np.float32),
    }
    nc = bacc.Bacc("TRN2", target_bir_lowering=False, num_devices=1)
    args = [nc.dram_tensor(f"in_{name}", t.shape, mybir.dt.from_np(t.dtype), kind="ExternalInput").ap()
            for name, t in arrays.items()]
    args.append(nc.dram_tensor("out", (B, SQ, D), F32, kind="ExternalOutput").ap())
    cross_attention_stack(nc, *args)
    r = run_bass_kernel_spmd(nc, [{f"in_{name}": t for name, t in arrays.items()}], core_ids=[0])
    return r.results[0]["out"]
```
